# Optimizing a Trainium2 kernel written in Bass

```python
import numpy as np
import jax
import jax.numpy as jnp

def _softmax(x, axis=-1):
    return jax.nn.softmax(x, axis=axis)
def _gelu(x):
    return jax.nn.gelu(x, approximate=True)
def _silu(x):
    return jax.nn.silu(x)
def _sigmoid(x):
    return jax.nn.sigmoid(x)
def _layernorm(x, axis=-1, eps=1e-5):
    m = jnp.mean(x, axis=axis, keepdims=True)
    v = jnp.var(x, axis=axis, keepdims=True)
    return (x - m) / jnp.sqrt(v + eps)
def _scatter_add(tgt, idx, src, axis=0):
    return tgt.at[idx].add(src)
def _segment_sum(src, seg, n):
    return jax.ops.segment_sum(src, seg, n)

kernel_name = 'mk_conv_preact_d2_conv_nhwc192_b1c6e3'

def setup_inputs(seed: int = 0):
    np.random.seed(seed)
    _w = jnp.asarray
    def _rec_inputs():
        import jax
        import jax.numpy as jnp
        _gk = jax.random.key(seed)
        x = -0.0002221 + 1 * jax.random.normal(jax.random.fold_in(_gk, 1), (2, 256, 256, 192), jnp.float32)
        return x
    x = _rec_inputs()
    def _L0_conv_setup():
        import jax, jax.numpy as jnp
        import numpy as np
        DN = ('NHWC', 'HWIO', 'NHWC')

        def _mdta(x, w_qkv, b_qkv, w_dw, b_dw, temperature, w_out, b_out):
            B, H, W, C = x.shape
            heads = temperature.shape[1]
            c = C // heads
            qkv = jax.lax.conv_general_dilated(x, w_qkv, (1, 1), 'SAME', dimension_numbers=DN) + b_qkv
            qkv = jax.lax.conv_general_dilated(qkv, w_dw, (1, 1), 'SAME', dimension_numbers=DN, feature_group_count=3 * C) + b_dw
            q, k, v = jnp.split(qkv, 3, axis=-1)

            def to_heads(t):
                return t.reshape(B, H * W, heads, c).transpose(0, 2, 3, 1)
            q, k, v = (to_heads(q), to_heads(k), to_heads(v))
            q = q / jnp.maximum(jnp.linalg.norm(q, axis=-1, keepdims=True), 1e-12)
            k = k / jnp.maximum(jnp.linalg.norm(k, axis=-1, keepdims=True), 1e-12)
            attn = jnp.einsum('bhcn,bhdn->bhcd', q, k) * temperature
            attn = jax.nn.softmax(attn, axis=-1)
            out = jnp.einsum('bhcd,bhdn->bhcn', attn, v)
            out = out.transpose(0, 3, 1, 2).reshape(B, H, W, C)
            out = jax.lax.conv_general_dilated(out, w_out, (1, 1), 'SAME', dimension_numbers=DN) + b_out
            return out
        key = jax.random.key(seed)
        ks = jax.random.split(key, 5)
        B, H, W, C = (2, 256, 256, 192)
        heads = 4
        x = jax.random.normal(ks[0], (B, H, W, C), dtype=jnp.float32)
        w_qkv = jax.random.normal(ks[1], (1, 1, C, 3 * C), dtype=jnp.float32) * 0.05
        b_qkv = jnp.zeros((3 * C,), dtype=jnp.float32)
        w_dw = jax.random.normal(ks[2], (3, 3, 1, 3 * C), dtype=jnp.float32) * 0.05
        b_dw = jnp.zeros((3 * C,), dtype=jnp.float32)
        temperature = jnp.ones((1, heads, 1, 1), dtype=jnp.float32)
        w_out = jax.random.normal(ks[3], (1, 1, C, C), dtype=jnp.float32) * 0.05
        b_out = jnp.zeros((C,), dtype=jnp.float32)
        return {'x': x, 'w_qkv': w_qkv, 'b_qkv': b_qkv, 'w_dw': w_dw, 'b_dw': b_dw, 'temperature': temperature, 'w_out': w_out, 'b_out': b_out}
    _L0_conv_all = _L0_conv_setup()
    _L0_conv_in = {k: v for k, v in _L0_conv_all.items() if k in ('w_qkv', 'b_qkv', 'w_dw', 'b_dw', 'temperature', 'w_out', 'b_out', )}
    del _L0_conv_all

    def _L1_conv_setup():
        import jax, jax.numpy as jnp
        import numpy as np
        from jax import lax
        DIM = 192

        def s6_scan(x, A, Bv, Cv, Dv, res_scale):
            N, L, C = x.shape
            h0 = jnp.zeros((N, C), dtype=x.dtype)
            dr = Dv + res_scale

            def step(h, xt):
                h = jnp.matmul(h, A) + Bv * xt
                y = Cv * h + dr * xt
                return (h, y)
            _, ys = lax.scan(step, h0, jnp.swapaxes(x, 0, 1))
            return jnp.swapaxes(ys, 0, 1)
        key = jax.random.key(seed)
        k1, k2, k3, k4, k5 = jax.random.split(key, 5)
        B, H, W, C = (8, 128, 128, DIM)
        x = jax.random.normal(k1, (B, H, W, C), dtype=jnp.float32)
        A = 0.05 * jax.random.normal(k2, (C, C), dtype=jnp.float32)
        Bv = jax.random.normal(k3, (C,), dtype=jnp.float32)
        Cv = jax.random.normal(k4, (C,), dtype=jnp.float32)
        Dv = jax.random.normal(k5, (C,), dtype=jnp.float32)
        res_scale = jnp.ones((1,), dtype=jnp.float32)
        return {'x': x, 'A': A, 'Bv': Bv, 'Cv': Cv, 'Dv': Dv, 'res_scale': res_scale}
    _L1_conv_all = _L1_conv_setup()
    _L1_conv_in = {k: v for k, v in _L1_conv_all.items() if k in ('A', 'Bv', 'Cv', 'Dv', 'res_scale', )}
    del _L1_conv_all

    return {
        "x": x,
        "L0_conv_w_qkv": _L0_conv_in["w_qkv"],
        "L0_conv_b_qkv": _L0_conv_in["b_qkv"],
        "L0_conv_w_dw": _L0_conv_in["w_dw"],
        "L0_conv_b_dw": _L0_conv_in["b_dw"],
        "L0_conv_temperature": _L0_conv_in["temperature"],
        "L0_conv_w_out": _L0_conv_in["w_out"],
        "L0_conv_b_out": _L0_conv_in["b_out"],
        "L1_conv_A": _L1_conv_in["A"],
        "L1_conv_Bv": _L1_conv_in["Bv"],
        "L1_conv_Cv": _L1_conv_in["Cv"],
        "L1_conv_Dv": _L1_conv_in["Dv"],
        "L1_conv_res_scale": _L1_conv_in["res_scale"],
    }

def reference(x, L0_conv_w_qkv, L0_conv_b_qkv, L0_conv_w_dw, L0_conv_b_dw, L0_conv_temperature, L0_conv_w_out, L0_conv_b_out, L1_conv_A, L1_conv_Bv, L1_conv_Cv, L1_conv_Dv, L1_conv_res_scale):
    import jax
    import jax.numpy as jnp
    def _L0_conv_ref(x, w_qkv, b_qkv, w_dw, b_dw, temperature, w_out, b_out):
        import jax, jax.numpy as jnp
        import numpy as np
        DN = ('NHWC', 'HWIO', 'NHWC')

        def _mdta(x, w_qkv, b_qkv, w_dw, b_dw, temperature, w_out, b_out):
            B, H, W, C = x.shape
            heads = temperature.shape[1]
            c = C // heads
            qkv = jax.lax.conv_general_dilated(x, w_qkv, (1, 1), 'SAME', dimension_numbers=DN) + b_qkv
            qkv = jax.lax.conv_general_dilated(qkv, w_dw, (1, 1), 'SAME', dimension_numbers=DN, feature_group_count=3 * C) + b_dw
            q, k, v = jnp.split(qkv, 3, axis=-1)

            def to_heads(t):
                return t.reshape(B, H * W, heads, c).transpose(0, 2, 3, 1)
            q, k, v = (to_heads(q), to_heads(k), to_heads(v))
            q = q / jnp.maximum(jnp.linalg.norm(q, axis=-1, keepdims=True), 1e-12)
            k = k / jnp.maximum(jnp.linalg.norm(k, axis=-1, keepdims=True), 1e-12)
            attn = jnp.einsum('bhcn,bhdn->bhcd', q, k) * temperature
            attn = jax.nn.softmax(attn, axis=-1)
            out = jnp.einsum('bhcd,bhdn->bhcn', attn, v)
            out = out.transpose(0, 3, 1, 2).reshape(B, H, W, C)
            out = jax.lax.conv_general_dilated(out, w_out, (1, 1), 'SAME', dimension_numbers=DN) + b_out
            return out
        return _mdta(x, w_qkv, b_qkv, w_dw, b_dw, temperature, w_out, b_out)

    def _L1_conv_ref(x, A, Bv, Cv, Dv, res_scale):
        import jax, jax.numpy as jnp
        import numpy as np
        from jax import lax
        DIM = 192

        def s6_scan(x, A, Bv, Cv, Dv, res_scale):
            N, L, C = x.shape
            h0 = jnp.zeros((N, C), dtype=x.dtype)
            dr = Dv + res_scale

            def step(h, xt):
                h = jnp.matmul(h, A) + Bv * xt
                y = Cv * h + dr * xt
                return (h, y)
            _, ys = lax.scan(step, h0, jnp.swapaxes(x, 0, 1))
            return jnp.swapaxes(ys, 0, 1)
        B, H, W, C = x.shape
        horiz = jnp.transpose(x, (0, 2, 1, 3)).reshape(B * W, H, C)
        y_h = s6_scan(horiz, A, Bv, Cv, Dv, res_scale).reshape(B, W, H, C)
        y_h = jnp.transpose(y_h, (0, 2, 1, 3))
        vert = x.reshape(B * H, W, C)
        y_v = s6_scan(vert, A, Bv, Cv, Dv, res_scale).reshape(B, H, W, C)
        dlen = min(H, W)
        idx = jnp.arange(dlen)
        diag_in = x[:, idx, idx, :]
        anti_in = x[:, idx, W - 1 - idx, :]
        diag_p = s6_scan(diag_in, A, Bv, Cv, Dv, res_scale)
        anti_p = s6_scan(anti_in, A, Bv, Cv, Dv, res_scale)
        zeros = jnp.zeros_like(x)
        diag_map = zeros.at[:, idx, idx, :].set(diag_p)
        anti_map = zeros.at[:, idx, W - 1 - idx, :].set(anti_p)
        return y_h + y_v + diag_map + anti_map

    def _gn(v, G=32, eps=1e-5):
        B_, H_, W_, C_ = v.shape
        g = v.reshape(B_, H_, W_, G, C_ // G)
        m = jnp.mean(g, axis=(1, 2, 4), keepdims=True)
        s = jnp.var(g, axis=(1, 2, 4), keepdims=True)
        return ((g - m) / jnp.sqrt(s + eps)).reshape(v.shape)

    def _ln_c(v, eps=1e-6):
        m = jnp.mean(v, axis=-1, keepdims=True)
        s = jnp.var(v, axis=-1, keepdims=True)
        return (v - m) / jnp.sqrt(s + eps)

    def _ln_t(v, eps=1e-5):
        m = jnp.mean(v, axis=-1, keepdims=True)
        s = jnp.var(v, axis=-1, keepdims=True)
        return (v - m) / jnp.sqrt(s + eps)

    def _to_tokens(v):
        B_, H_, W_, C_ = v.shape
        return v.reshape(B_, H_ * W_, C_)
    def _from_tokens(t, like):
        return t.reshape(like.shape)

    x = x + _L0_conv_ref(_gn(x), L0_conv_w_qkv, L0_conv_b_qkv, L0_conv_w_dw, L0_conv_b_dw, L0_conv_temperature, L0_conv_w_out, L0_conv_b_out)
    x = x + _L1_conv_ref(_gn(x), L1_conv_A, L1_conv_Bv, L1_conv_Cv, L1_conv_Dv, L1_conv_res_scale)
    return x


_drawn_inputs = setup_inputs


def setup_inputs(seed=0):
    import zlib

    import numpy as np

    out = dict(_drawn_inputs(seed))
    spreads = {'L0_conv_b_qkv': (0.0, 0.8),
     'L0_conv_b_dw': (0.0, 0.8),
     'L0_conv_temperature': (1.0, 0.6),
     'L0_conv_b_out': (0.0, 0.1)}
    factors = {'L0_conv_w_qkv': 5.416, 'L0_conv_w_dw': 5.417, 'L0_conv_w_out': 4.467}
    for name, (base, spread) in spreads.items():
        noise = np.random.default_rng([zlib.crc32(name.encode()), seed]).standard_normal(out[name].shape)
        drawn = base * np.exp(spread * noise) if base else spread * noise
        out[name] = jnp.asarray(drawn.astype(out[name].dtype))
    for name, factor in factors.items():
        out[name] = (out[name] * factor).astype(out[name].dtype)
    return out
```

```python
import numpy as np
import concourse.bass as bass
from concourse import mybir
from contextlib import ExitStack

F32 = mybir.dt.float32
BF16 = mybir.dt.bfloat16
ALU = mybir.AluOpType
ACT = mybir.ActivationFunctionType
AX = mybir.AxisListType

C = 192
KC = 96
B = 2
R = 8
GROUP = 6
VEC_TAP, VEC_BQKV, VEC_BDW = 0, 9, 10
V_BV, V_CV, V_DV, V_BOUT, V_TEMP, V_RES = range(6)
PSUM_BANK = 512


def group_norm_scale(nc, block, raw, mean_sq_ready, group_sum, tmp, scale, shift, gavg, eps, sems):
    s_avg, s_var, s_std, s_done = sems

    @block.tensor
    def _(pe):
        pe.wait_ge(mean_sq_ready[0], mean_sq_ready[1])
        nc.tensor.matmul(group_sum[0:KC, 0:8], gavg[:, :], raw[:, :, :], start=True, stop=True).then_inc(s_avg, 1)

    @block.vector
    def _(dve):
        dve.wait_ge(s_avg, 1)
        g = group_sum[0:KC, 0:8].rearrange("p (a m) -> p a m", m=2)
        nc.vector.tensor_copy(tmp[:, 0:4], g[:, :, 0]).then_inc(s_done, 1)
        dve.wait_ge(s_done, 1)
        nc.vector.tensor_tensor(tmp[:, 4:8], tmp[:, 0:4], tmp[:, 0:4], ALU.mult).then_inc(s_done, 1)
        dve.wait_ge(s_done, 2)
        nc.vector.tensor_tensor(tmp[:, 8:12], g[:, :, 1], tmp[:, 4:8], ALU.subtract).then_inc(s_done, 1)
        dve.wait_ge(s_done, 3)
        nc.vector.tensor_scalar_add(tmp[:, 12:16], tmp[:, 8:12], eps).then_inc(s_var, 1)
        dve.wait_ge(s_std, 1)
        nc.vector.reciprocal(scale[:, :], tmp[:, 16:20]).then_inc(s_done, 1)
        dve.wait_ge(s_done, 4)
        nc.vector.scalar_tensor_tensor(shift[:, :], tmp[:, 0:4], -1.0, scale[:, :], ALU.mult, ALU.mult).then_inc(s_done, 1)
        dve.wait_ge(s_done, 5)

    @block.scalar
    def _(act):
        act.wait_ge(s_var, 1)
        nc.scalar.activation(tmp[:, 16:20], tmp[:, 12:16], ACT.Sqrt).then_inc(s_std, 1)


def build(nc, x_cm, x_px, w_qkv, w_out, a_mat, vec128, vec96, select, gavg_d, mask_d, x1_d, part_d, out, H, W):
    NPX = R * W
    UNITS = NPX // PSUM_BANK
    UR = PSUM_BANK // W
    NCH = H // R
    PT = NPX // 128
    YW = W + 2
    HT = W // 128
    assert H == W and NCH % 2 == 0 and NCH >= 6

    outer = ExitStack()

    names = {}

    def unique(name):
        names[name] = names.get(name, 0) + 1
        return name if names[name] == 1 else f"{name}_{names[name]}"

    def sb(ctx, name, shape, dt=F32):
        return ctx.enter_context(nc.sbuf_tensor(unique(name), shape, dt))

    def pb(ctx, name, shape):
        return ctx.enter_context(nc.psum_tensor(unique(name), shape, F32))

    live = []

    def sem(name):
        live.append(nc.alloc_semaphore(name=unique("s_" + name)))
        return live[-1]

    def end_phase():
        nc.clear_and_free_semaphores(live)
        nc.all_engine_barrier()
        live.clear()

    def loop(eng, n, body):
        body(0, True, False)
        with eng.Fori(1, n - 1) as i:
            body(i, False, False)
        body(n - 1, False, True)

    with outer:
        sel = sb(outer, "sel", [128, 3, 384])
        gavg = sb(outer, "gavg", [KC, KC])
        mask = sb(outer, "mask", [KC, KC])
        v128 = sb(outer, "v128", [128, 5, 11])
        v96 = sb(outer, "v96", [KC, 2, 6])
        amat = sb(outer, "amat", [KC, 2, C])
        wout = sb(outer, "wout", [KC, 2, C])
        scale1 = sb(outer, "scale1", [KC, 4])
        shift1 = sb(outer, "shift1", [KC, 4])
        scale2 = sb(outer, "scale2", [KC, 4])
        shift2 = sb(outer, "shift2", [KC, 4])
        gn_tmp = sb(outer, "gn_tmp", [KC, 20])
        moments = sb(outer, "moments", [KC, 4, 2])
        ident = sel[:, 0, 0:128]
        x1_sq = sb(outer, "x1_sq", [KC, 4])
        x1_mean = sb(outer, "x1_mean", [KC, 4])

        with ExitStack() as conv:
            wraw = sb(conv, "wraw", [KC, 2, 3 * C])
            wfold = [sb(conv, f"wfold{b}", [KC, 2, 3 * C]) for b in range(B)]
            bias_y = sb(conv, "bias_y", [128, 4, 2])
            bias_yc = sb(conv, "bias_yc", [128, 1])
            x_in = [sb(conv, f"x_in{s}", [KC, 2, NPX]) for s in range(2)]
            y = [[sb(conv, f"y{s}_{j}", [128, R + 2, YW]) for j in range(3)] for s in range(2)]
            acc = [[sb(conv, f"acc{s}_{j}", [128, NPX]) for j in range(3)] for s in range(2)]
            mix_a = [sb(conv, f"mix_a{b}", [128, C]) for b in range(B)]
            mix_c = [sb(conv, f"mix_c{b}", [128, C]) for b in range(B)]

            stats_phase(nc, sb, pb, sem, loop, 
                NPX=NPX, UNITS=UNITS, NCH=NCH, x_cm=x_cm, x_in=x_in, acc=acc, y=y, sel=sel, gavg=gavg, mask=mask,
                v128=v128, v96=v96, amat=amat, wout=wout, wraw=wraw, wfold=wfold, bias_y=bias_y, bias_yc=bias_yc,
                scale=scale1, shift=shift1, gn_tmp=gn_tmp, moments=moments, w_qkv=w_qkv, w_out=w_out, a_mat=a_mat,
                vec128=vec128, vec96=vec96, select=select, gavg_d=gavg_d, mask_d=mask_d)
            end_phase()

            for b in range(B):
                with ExitStack() as qk:
                    gram = sb(qk, "gram", [KC, 2, KC])
                    sq_norm = sb(qk, "sq_norm", [128, 3, NCH])
                    qk_phase(nc, sb, pb, sem, loop, 
                        b=b, NPX=NPX, UNITS=UNITS, UR=UR, NCH=NCH, PT=PT, H=H, W=W, x_cm=x_cm, x_in=x_in, y=y, acc=acc,
                        wfold=wfold[b], bias_y=bias_y, v128=v128, ident=ident, gram=gram, sq_norm=sq_norm)
                    attention_phase(nc, sb, pb, sem, 
                        b=b, NCH=NCH, gram=gram, sq_norm=sq_norm, sel=sel, mask=mask, v96=v96, wout=wout,
                        mix_a=mix_a[b], mix_c=mix_c[b])
                    end_phase()

            v_phase(nc, sb, pb, sem, loop, 
                NPX=NPX, UNITS=UNITS, UR=UR, NCH=NCH, PT=PT, H=H, W=W, x_cm=x_cm, x_px=x_px, x1_d=x1_d, x_in=x_in,
                y=y, acc=acc, wfold=wfold, bias_y=bias_y, bias_yc=bias_yc, v128=v128, mix_a=mix_a, mix_c=mix_c,
                x1_sq=x1_sq, x1_mean=x1_mean, moments=moments)
            end_phase()

        with ExitStack() as scan:
            co = {n: sb(scan, n, [KC, 4]) for n in ("u_mul", "u_add", "e_mul", "e_add", "d_mul", "d_add", "c_tmp", "c_base")}
            scan_coefficients(nc, sb, pb, sem, 
                H=H, W=W, x1_sq=x1_sq, x1_mean=x1_mean, v96=v96, gavg=gavg, scale=scale2, shift=shift2, gn_tmp=gn_tmp,
                moments=moments, co=co)
            for vertical in (False, True):
                scan_phase(nc, sb, pb, sem, loop, 
                    along_w=vertical, H=H, W=W, HT=HT, x1_d=x1_d, part_d=part_d, out=out, amat=amat, v96=v96, co=co, ident=ident)
                end_phase()


def stats_phase(nc, sb, pb, sem, loop, *, NPX, UNITS, NCH, x_cm, x_in, acc, y, sel, gavg, mask, v128, v96, amat, wout,
                wraw, wfold, bias_y, bias_yc, scale, shift, gn_tmp, moments, w_qkv, w_out, a_mat, vec128, vec96, select,
                gavg_d, mask_d):
    s_const, s_side = sem("p1_const"), sem("p1_side")
    slots = [[x_in[s][:, k, :] for k in range(2)] for s in range(2)] + [[acc[s][k][0:KC, :] for k in range(2)] for s in range(2)]
    NS = len(slots)
    assert NCH % NS == 0
    s_load = [sem(f"p1_load{s}") for s in range(NS)]
    s_used, s_dve, s_mom = sem("p1_used"), sem("p1_dve"), sem("p1_mom")
    gn_sems = [sem(f"p1_gn{i}") for i in range(4)]
    with ExitStack() as ctx:
        stats = [sb(ctx, f"bn_stats{b}", [KC, 2, NCH * UNITS, 6]) for b in range(B)]
        mv = sb(ctx, "bn_mv", [KC, 4, 2])
        ps = pb(ctx, "p1_ps", [128, 16])
        with nc.Block() as block:
            @block.sync
            def _(sp):
                for dst, src in ((wraw, w_qkv), (wout, w_out), (amat, a_mat), (v128, vec128),
                                 (v96, vec96), (sel, select)):
                    sp.dma_start(dst[:, :, :], src).then_inc(s_const, 16)
                sp.dma_start(gavg[:, :], gavg_d).then_inc(s_const, 16)
                sp.dma_start(mask[:, :], mask_d).then_inc(s_const, 16)
                for b in range(B):
                    src = x_cm[b].rearrange("(k c) n -> c k n", k=2)

                    def body(i, first, last):
                        for s in range(NS):
                            if not (first and b == 0):
                                sp.wait_ge(s_used, b * NCH + NS * i + s - NS + 1)
                            for k in range(2):
                                sp.dma_start(slots[s][k], src[:, k, bass.ds((NS * i + s) * NPX, NPX)]).then_inc(s_load[s], 16)
                    loop(sp, NCH // NS, body)
                sp.wait_ge(s_const, 16 * 8)

            @block.gpsimd
            def _(pool):
                for s in range(2):
                    for j in range(3):
                        nc.gpsimd.memset(y[s][j][:, :, :], 0.0).then_inc(s_side, 1)
                pool.wait_ge(s_side, 6)

            @block.vector
            def _(dve):
                for b in range(B):
                    def body(i, first, last):
                        for s in range(NS):
                            dve.wait_ge(s_load[s], 32 * (b * (NCH // NS) + i + 1))
                            for k in range(2):
                                for u in range(UNITS):
                                    ins = nc.vector.bn_stats(
                                        stats[b][:, k, bass.ds((NS * i + s) * UNITS + u, 1), :].rearrange("p a c -> p (a c)"),
                                        slots[s][k][:, u * 512:(u + 1) * 512])
                            ins.then_inc(s_used, 1)
                    loop(dve, NCH // NS, body)
                dve.wait_ge(s_used, B * NCH)
                for b in range(B):
                    for k in range(2):
                        nc.vector.bn_aggr(mv[:, 2 * k + b, :], stats[b][:, k, :, :].rearrange("p a c -> p (a c)")).then_inc(s_dve, 1)
                dve.wait_ge(s_dve, 4)
                nc.vector.tensor_tensor(moments[:, :, 0], mv[:, :, 0], mv[:, :, 0], ALU.mult).then_inc(s_dve, 1)
                dve.wait_ge(s_dve, 5)
                nc.vector.tensor_tensor(moments[:, :, 1], mv[:, :, 1], moments[:, :, 0], ALU.add).then_inc(s_dve, 1)
                dve.wait_ge(s_dve, 6)
                nc.vector.tensor_copy(moments[:, :, 0], mv[:, :, 0]).then_inc(s_mom, 1)

        with nc.Block() as block:
            group_norm_scale(nc, block, moments, (s_mom, 1), ps, gn_tmp, scale, shift, gavg, 1e-5, gn_sems)

        s_bias, s_fold = sem("p1_bias"), sem("p1_fold")
        with nc.Block() as block:
            @block.tensor
            def _(pe):
                for j in range(4):
                    for k in range(2):
                        nc.tensor.matmul(ps[:, 2 * j:2 * j + 2], wraw[:, k, 128 * j:128 * j + 128], shift[:, 2 * k:2 * k + 2],
                                         start=(k == 0), stop=(k == 1))
                for b in range(B):
                    for k in range(2):
                        ins = nc.tensor.matmul(ps[64 * b:64 * b + 64, 8:9], wraw[:, k, 512:576], shift[:, 2 * k + b:2 * k + b + 1],
                                               start=(k == 0), stop=(k == 1))
                ins.then_inc(s_bias, 1)

            @block.vector
            def _(dve):
                for b in range(B):
                    for k in range(2):
                        nc.vector.tensor_scalar(wfold[b][:, k, :], wraw[:, k, :], scale[:, 2 * k + b:2 * k + b + 1], None,
                                                ALU.mult).then_inc(s_fold, 1)
                dve.wait_ge(s_bias, 1)
                for j in range(4):
                    nc.vector.tensor_scalar(bias_y[:, j, :], ps[:, 2 * j:2 * j + 2], v128[:, j, VEC_BQKV:VEC_BQKV + 1], None,
                                            ALU.add).then_inc(s_fold, 1)
                nc.vector.tensor_tensor(bias_yc[:, :], ps[:, 8:9], v128[:, 4, VEC_BQKV:VEC_BQKV + 1], ALU.add).then_inc(s_fold, 1)
                dve.wait_ge(s_fold, 9)


PE_TAPS = ((0, 0), (0, 1))
DVE_TAPS = tuple((dy, dx) for dy in range(3) for dx in range(3) if (dy, dx) not in PE_TAPS)


def qk_phase(nc, sb, pb, sem, loop, *, b, NPX, UNITS, UR, NCH, PT, H, W, x_cm, x_in, y, acc, wfold, bias_y, v128, ident,
             gram, sq_norm):
    NU = 3 * UNITS
    NT = len(DVE_TAPS)
    p = f"qk{b}_"
    s_row0, s_diag = sem(p + "row0"), sem(p + "diag")
    s_load = [sem(f"{p}load{s}") for s in range(2)]
    s_y, s_yev = sem(p + "y_ready"), sem(p + "y_evicted")
    s_edge = sem(p + "edge_rows")
    s_tap, s_acc = sem(p + "taps_ready"), sem(p + "acc_started")
    s_dw = sem(p + "dw_ops")
    s_t, s_tev = sem(p + "transposed"), sem(p + "transposed_evicted")
    s_gram, s_gadd, s_sq = sem(p + "gram_tile"), sem(p + "gram_added"), sem(p + "squared")
    with ExitStack() as ctx:
        x_row0 = sb(ctx, "x_row0", [KC, 2, W])
        diag = sb(ctx, "diag", [128, 3, len(PE_TAPS), 128])
        qk_t = [sb(ctx, f"qk_t{s}", [128, 384]) for s in range(4)]
        junk = sb(ctx, "junk", [128, NPX], BF16)
        y_ps = [pb(ctx, f"y_ps{s}", [128, 512]) for s in range(2)]
        tap_ps = [pb(ctx, f"tap_ps{s}", [128, 512]) for s in range(2)]
        t_ps = [pb(ctx, f"t_ps{s}", [128, 512]) for s in range(2)]
        gram_ps = [pb(ctx, f"gram_ps{s}", [128, 512]) for s in range(2)]
        tiles_after = [range(u * PT // NU, (u + 1) * PT // NU) for u in range(NU)]

        def yview(t, dy, dx, r0, rows):
            return t[:, dy + r0:dy + r0 + rows, dx:dx + W]

        with nc.Block() as block:
            @block.sync
            def _(sp):
                src = x_cm[b].rearrange("(k c) n -> c k n", k=2)
                sp.dma_start(x_row0[:, :, :], src[:, :, 0:W]).then_inc(s_row0, 16)

                def body(i, first, last):
                    for s in range(2):
                        if not first:
                            sp.wait_ge(s_y, 3 + NU * (2 * i + s - 1))
                        sp.dma_start(x_in[s][:, :, :], src[:, :, bass.ds((2 * i + s) * NPX + W, NPX)]).then_inc(s_load[s], 16)
                loop(sp, NCH // 2, body)

            @block.gpsimd
            def _(pool):
                for j in range(3):
                    nc.gpsimd.memset(y[0][j][:, 0, :], 0.0).then_inc(s_edge, 1)

                pool.wait_ge(s_yev, 3 + NU * NCH)
                for j in range(3):
                    nc.gpsimd.memset(y[1][j][:, R + 1, :], 0.0).then_inc(s_edge, 1)

            @block.tensor
            def _(pe):
                def project(j, u, dst, xt, n):
                    for k in range(2):
                        ins = nc.tensor.matmul(dst[:, 0:n], wfold[:, k, 128 * j:128 * j + 128],
                                               xt[:, k, u * 512:u * 512 + n], start=(k == 0), stop=(k == 1))
                    ins.then_inc(s_y, 1)

                def conv_unit(c, s, u, skip_wait):
                    if not skip_wait:
                        pe.wait_ge(s_yev, NU * c + u + 3 - 1)
                    project(u // UNITS, u % UNITS, y_ps[(u + 3) % 2], x_in[s], 512)

                def transpose_tile(c, s, t, skip_wait):
                    if not skip_wait:
                        pe.wait_ge(s_tev, PT * c + t - 1)
                    for j in range(3):
                        ins = nc.tensor.transpose(t_ps[t % 2][:, 128 * j:128 * j + 128], acc[s][j][:, 128 * t:128 * t + 128], ident)
                    ins.then_inc(s_t, 1)

                def gram_tile(c, s, t):
                    pe.wait_ge(s_tev, PT * c + t + 1)
                    for hp in range(2):
                        ins = nc.tensor.matmul(gram_ps[s][0:KC, KC * hp:KC * hp + KC], qk_t[t % 4][:, KC * hp:KC * hp + KC],
                                               qk_t[t % 4][:, C + KC * hp:C + KC * hp + KC], start=(t == 0 and hp == 0),
                                               stop=(t == PT - 1 and hp == 1), skip_group_check=True)
                    ins.then_inc(s_gram, 1)

                def gram_step(c, s, t, first):
                    transpose_tile(c, s, t, first and t < 2)
                    if t >= 2:
                        gram_tile(c, s, t - 2)

                def gram_begin(c, early):
                    pe.wait_ge(s_dw, 3 * NT * (c + 1))
                    if not early:
                        pe.wait_ge(s_gadd, c)

                def taps(c, s, first):
                    for u in range(NU):
                        j, q = u // UNITS, u % UNITS
                        if q == 0:
                            pe.wait_ge(s_yev, 3 + NU * c + UNITS * (j + 1))
                        if u == 0:
                            pe.wait_ge(s_edge, 3 * (c + 1))
                        if not (first and u < 2):
                            pe.wait_ge(s_acc, NU * c + u - 1)
                        for n, (dy, dx) in enumerate(PE_TAPS):
                            ins = nc.tensor.matmul(tap_ps[u % 2][:, :], diag[:, j, n, :], yview(y[s][j], dy, dx, q * UR, UR),
                                                   start=(n == 0), stop=(n == len(PE_TAPS) - 1))
                        ins.then_inc(s_tap, 1)

                pe.wait_ge(s_row0, 16)
                for j in range(3):
                    if j == 2:
                        pe.wait_ge(s_yev, 1)
                    project(j, 0, y_ps[j % 2], x_row0, W)
                pe.wait_ge(s_load[0], 16)
                for u in range(NU):
                    conv_unit(0, 0, u, False)
                pe.wait_ge(s_diag, 3 * len(PE_TAPS))
                taps(0, 0, True)

                def body(i, first, last):
                    for s in range(2):
                        c = 2 * i + s
                        has_next = not (last and s == 1)
                        has_prev = not (first and s == 0)
                        step(c, i, s, has_next, has_prev, first and s == 1, first)

                def step(c, i, s, has_next, has_prev, prev_first, early):
                    if has_next:
                        pe.wait_ge(s_load[1 - s], 16 * (i + 1 + s))
                    if has_prev:
                        gram_begin(c - 1, early)
                    for u in range(NU):
                        if has_next:
                            conv_unit(c + 1, 1 - s, u, False)
                        if has_prev:
                            for t in tiles_after[u]:
                                gram_step(c - 1, 1 - s, t, prev_first)
                    if has_prev:
                        for t in (PT - 2, PT - 1):
                            gram_tile(c - 1, 1 - s, t)
                    if has_next:
                        taps(c + 1, 1 - s, False)
                loop(pe, NCH // 2, body)
                gram_begin(NCH - 1, False)
                for t in range(PT):
                    gram_step(NCH - 1, 1, t, False)
                for t in (PT - 2, PT - 1):
                    gram_tile(NCH - 1, 1, t)

            @block.scalar
            def _(act):
                def evict_y(c, s, u):
                    j, q = u // UNITS, u % UNITS
                    act.wait_ge(s_y, 3 + NU * c + u + 1)
                    nc.scalar.activation(y[s][j][:, 2 + q * UR:2 + q * UR + UR, 1:W + 1],
                                         y_ps[(u + 3) % 2][:, :].rearrange("p (r w) -> p r w", w=W), ACT.Identity,
                                         bias=bias_y[:, j, b:b + 1]).then_inc(s_yev, 1)

                def evict_t(c, t, first_use):
                    act.wait_ge(s_t, PT * c + t + 1)
                    if not (first_use and t < 4):
                        act.wait_ge(s_gram, PT * c + t - 3)
                    nc.scalar.activation(qk_t[t % 4][:, :], t_ps[t % 2][:, 0:384], ACT.Copy).then_inc(s_tev, 1)

                def evict_taps(c, s):
                    for u in range(NU):
                        j, q = u // UNITS, u % UNITS
                        act.wait_ge(s_tap, NU * c + u + 1)
                        nc.scalar.activation(acc[s][j][:, q * 512:(q + 1) * 512], tap_ps[u % 2][:, :], ACT.Identity,
                                             bias=v128[:, j, VEC_BDW:VEC_BDW + 1]).then_inc(s_acc, 1)

                def squares(c, s, tiles=range(3)):
                    act.wait_ge(s_dw, 3 * NT * (c + 1))
                    for j in tiles:
                        act.wait_ge(s_sq, 3 * c + j)
                        nc.scalar.activation(junk[:, :], acc[s][j][:, :], ACT.Square,
                                             accum_out=sq_norm[:, j, bass.ds(c, 1)]).then_inc(s_sq, 1)

                for j in range(3):
                    act.wait_ge(s_y, j + 1)
                    nc.scalar.activation(y[0][j][:, 1, 1:W + 1], y_ps[j % 2][:, 0:W], ACT.Identity,
                                         bias=bias_y[:, j, b:b + 1]).then_inc(s_yev, 1)
                for u in range(NU):
                    evict_y(0, 0, u)
                evict_taps(0, 0)

                def body(i, first, last):
                    for s in range(2):
                        c = 2 * i + s
                        has_next = not (last and s == 1)
                        has_prev = not (first and s == 0)
                        if has_next:
                            if has_prev:
                                act.wait_ge(s_dw, 3 * NT * c)
                            act.wait_ge(s_yev, 3 + NU * (c + 1))
                            for j in range(3):
                                nc.scalar.activation(y[1 - s][j][:, 0:2, 1:W + 1], y[s][j][:, R:R + 2, 1:W + 1], ACT.Copy).then_inc(s_edge, 1)
                        for u in range(NU):
                            if has_next:
                                evict_y(c + 1, 1 - s, u)
                            if has_prev:
                                for t in tiles_after[u]:
                                    evict_t(c - 1, t, first and s == 1)
                                if u % UNITS == 1:
                                    squares(c - 1, 1 - s, (u // UNITS,))
                        if has_next:
                            if has_prev:
                                act.wait_ge(s_t, PT * c)
                                act.wait_ge(s_sq, 3 * c)
                            evict_taps(c + 1, 1 - s)
                loop(act, NCH // 2, body)
                squares(NCH - 1, 1)
                for t in range(PT):
                    evict_t(NCH - 1, t, False)

            @block.vector
            def _(dve):
                for j in range(3):
                    for n, (dy, dx) in enumerate(PE_TAPS):
                        tap = 3 * dy + dx
                        nc.vector.tensor_scalar(diag[:, j, n, :], ident, v128[:, j, VEC_TAP + tap:VEC_TAP + tap + 1], None,
                                                ALU.mult).then_inc(s_diag, 1)
                nc.vector.memset(gram[:, :, :], 0.0).then_inc(s_gadd, 1)

                def add_gram(c, s):
                    dve.wait_ge(s_gram, PT * (c + 1))
                    dve.wait_ge(s_gadd, c + 1)
                    nc.vector.tensor_tensor(gram[:, :, :], gram_ps[s][0:KC, 0:C].rearrange("p (a n) -> p a n", a=2), gram[:, :, :],
                                            ALU.add).then_inc(s_gadd, 1)

                def body(i, first, last):
                    for s in range(2):
                        c = 2 * i + s
                        dve.wait_ge(s_edge, 3 * (c + 1) + (3 if last and s == 1 else 0))
                        for n, (dy, dx) in enumerate(DVE_TAPS):
                            for j in range(3):
                                if n == 0:
                                    dve.wait_ge(s_acc, NU * c + UNITS * (j + 1))
                                else:
                                    dve.wait_ge(s_dw, 3 * NT * c + 3 * (n - 1) + j + 1)
                                tap = 3 * dy + dx
                                a = acc[s][j][:, :].rearrange("p (r w) -> p r w", w=W)
                                nc.vector.scalar_tensor_tensor(a, yview(y[s][j], dy, dx, 0, R),
                                                               v128[:, j, VEC_TAP + tap:VEC_TAP + tap + 1], a,
                                                               ALU.mult, ALU.add).then_inc(s_dw, 1)
                            if n == 1 and not first:
                                add_gram(c - 2, s)
                loop(dve, NCH // 2, body)
                add_gram(NCH - 2, 0)
                add_gram(NCH - 1, 1)
                dve.wait_ge(s_gadd, NCH + 1)


def attention_phase(nc, sb, pb, sem, *, b, NCH, gram, sq_norm, sel, mask, v96, wout, mix_a, mix_c):
    p = f"at{b}_"
    s_dve, s_root, s_norm, s_exp, s_mix = sem(p + "dve"), sem(p + "root"), sem(p + "norms"), sem(p + "exp"), sem(p + "mix")
    s_nsq, s_rn, s_neg, s_prob = sem(p + "norm_sq"), sem(p + "rnorm"), sem(p + "neg_max"), sem(p + "probs")
    with ExitStack() as ctx:
        nsq = sb(ctx, "nsq", [128, 3])
        root = sb(ctx, "root", [128, 3])
        rn = sb(ctx, "rn", [128, 3])
        ones = sb(ctx, "at_ones", [128, KC])
        rn_rows = sb(ctx, "rn_rows", [128, 3, KC])
        rq = sb(ctx, "rq", [KC, 2])
        rk = sb(ctx, "rk", [KC, 2, KC])
        logit = sb(ctx, "logit", [KC, 2, KC])
        top = sb(ctx, "top", [KC, 2])
        neg = sb(ctx, "neg", [KC, 2])
        prob = sb(ctx, "prob", [KC, 2, KC])
        total = sb(ctx, "total", [KC, 2])
        rtotal = sb(ctx, "rtotal", [KC, 2])
        ps_k = pb(ctx, "ps_k", [128, 512])
        ps_q = pb(ctx, "ps_q", [128, 512])
        ps_a = pb(ctx, "ps_a", [128, 512])
        ps_c = pb(ctx, "ps_c", [128, 512])
        half = slice(64 * b, 64 * b + 64)
        with nc.Block() as block:
            @block.tensor
            def _(pe):
                pe.wait_ge(s_rn, 1)
                for j in range(3):
                    nc.tensor.matmul(ps_k[0:KC, 0:C], rn_rows[:, j, :], sel[:, j, C:2 * C], start=(j == 0), stop=(j == 2))
                for hp in range(2):
                    for j in range(3):
                        ins = nc.tensor.matmul(ps_q[0:KC, hp:hp + 1], sel[:, j, KC * hp:KC * hp + KC], rn[:, j:j + 1],
                                               start=(j == 0), stop=(j == 2))
                ins.then_inc(s_norm, 1)
                pe.wait_ge(s_prob, 2)
                nc.tensor.matmul(ps_a[0:96, 0:C], prob[:, 0, :], wout[:, 0, :], start=True, stop=True)
                nc.tensor.matmul(ps_a[96:128, 0:C], prob[:, 1, 0:32], wout[:, 1, :], start=True, stop=True)
                nc.tensor.matmul(ps_c[half, 0:C], prob[:, 1, 32:96], wout[:, 1, :], start=True, stop=True).then_inc(s_mix, 1)

            @block.scalar
            def _(act):
                act.wait_ge(s_nsq, 1)
                nc.scalar.activation(root[:, :], nsq[:, :], ACT.Sqrt).then_inc(s_root, 1)
                act.wait_ge(s_neg, 1)
                for hp in range(2):
                    nc.scalar.activation(prob[:, hp, :], logit[:, hp, :], ACT.Exp, bias=neg[:, hp:hp + 1],
                                         accum_out=total[:, hp:hp + 1]).then_inc(s_exp, 1)

            @block.vector
            def _(dve):
                n = [0]

                def link(ins):
                    n[0] += 1
                    ins.then_inc(s_dve, 1)
                    dve.wait_ge(s_dve, n[0])
                link(nc.vector.memset(ones[:, :], 1.0))
                link(nc.vector.memset(mix_c[:, :], 0.0))
                nc.vector.reduce_sum(nsq[:, :], sq_norm[:, :, :], AX.X).then_inc(s_nsq, 1)
                dve.wait_ge(s_root, 1)
                link(nc.vector.tensor_scalar_max(root[:, :], root[:, :], 1e-12))
                link(nc.vector.reciprocal(rn[:, :], root[:, :]))
                for j in range(3):
                    ins = nc.vector.tensor_scalar(rn_rows[:, j, :], ones[:, :], rn[:, j:j + 1], None, ALU.mult)
                ins.then_inc(s_rn, 1)
                dve.wait_ge(s_norm, 1)
                link(nc.vector.tensor_copy(rk[:, :, :], ps_k[0:KC, 0:C].rearrange("p (a n) -> p a n", a=2)))
                link(nc.vector.tensor_tensor(rq[:, :], ps_q[0:KC, 0:2], v96[:, :, V_TEMP], ALU.mult))
                for hp in range(2):
                    link(nc.vector.scalar_tensor_tensor(logit[:, hp, :], gram[:, hp, :], rq[:, hp:hp + 1], rk[:, hp, :],
                                                        ALU.mult, ALU.mult))
                    link(nc.vector.tensor_tensor(logit[:, hp, :], logit[:, hp, :], mask[:, :], ALU.add))
                    link(nc.vector.reduce_max(top[:, hp:hp + 1], logit[:, hp, :], AX.X))
                nc.vector.tensor_scalar(neg[:, :], top[:, :], -1.0, None, ALU.mult).then_inc(s_neg, 1)
                dve.wait_ge(s_exp, 2)
                link(nc.vector.reciprocal(rtotal[:, :], total[:, :]))
                for hp in range(2):
                    nc.vector.tensor_scalar(prob[:, hp, :], prob[:, hp, :], rtotal[:, hp:hp + 1], None, ALU.mult).then_inc(s_prob, 1)
                dve.wait_ge(s_mix, 1)
                link(nc.vector.tensor_copy(mix_a[:, :], ps_a[:, 0:C]))
                link(nc.vector.tensor_copy(mix_c[half, :], ps_c[half, 0:C]))


V_TAPS = tuple((dy, dx) for dy in range(3) for dx in range(3) if (dy, dx) != (0, 0))


def v_phase(nc, sb, pb, sem, loop, *, NPX, UNITS, UR, NCH, PT, H, W, x_cm, x_px, x1_d, x_in, y, acc, wfold, bias_y,
            bias_yc, v128, mix_a, mix_c, x1_sq, x1_mean, moments):
    NU = 3 * UNITS
    NT = len(V_TAPS)
    HPX = NPX // 2
    HU = UNITS // 2
    QT = PT // 2
    MU = B * PT // 2
    QM = QT // 2
    s_row0, s_one, s_edge = sem("v_row0"), sem("v_ones"), sem("v_edge_rows")
    s_load = [sem(f"v_load{s}") for s in range(2)]
    s_res = [sem(f"v_residual{s}") for s in range(4)]
    s_store = [sem(f"v_store{s}") for s in range(4)]
    s_y, s_yev = sem("v_y_ready"), sem("v_y_evicted")
    s_acc, s_dw = sem("v_acc_started"), sem("v_dw_ops")
    s_mix, s_x1, s_sq, s_st, s_sadd = sem("v_mixed"), sem("v_x1"), sem("v_squared"), sem("v_stat_units"), sem("v_sums_added")
    with ExitStack() as ctx:
        x_row0 = sb(ctx, "v_x_row0", [KC, 2, B, W])
        res = [sb(ctx, f"res{s}", [128, QT, C]) for s in range(4)]
        sq = [sb(ctx, f"sq{s}", [128, 2, C]) for s in range(4)]
        ones = sb(ctx, "v_ones", [128, 1])
        v_sums = sb(ctx, "v_sums", [128, 3, NCH])
        v_total = sb(ctx, "v_total", [128, 3])
        y_ps = [pb(ctx, f"vy_ps{s}", [128, 512]) for s in range(2)]
        mix_ps = [pb(ctx, f"mix_ps{s}", [128, 512]) for s in range(4)]
        st_ps = [pb(ctx, f"st_ps{s}", [128, 512]) for s in range(2)]
        x_half = [x_in[s][:, :, :].rearrange("c k (b n) -> c k b n", b=B) for s in range(2)]
        mix_after = [range(u * MU // NU, (u + 1) * MU // NU) for u in range(NU)]
        order = [(h, q, j) for h in range(2) for q in range(HU) for j in range(3)]

        def image_of(m):
            quarter, r = m // QM, m % QM
            h, b = quarter // 2, quarter % 2
            return quarter, b, h * HPX + r * 256, r

        with nc.Block() as block:
            @block.sync
            def _(sp):
                src = [x_cm[b].rearrange("(k c) n -> c k n", k=2) for b in range(B)]
                px = [x_px[b].rearrange("(t p) c -> p t c", p=128) for b in range(B)]
                dst = [x1_d[b].rearrange("(t p) c -> p t c", p=128) for b in range(B)]
                for b in range(B):
                    sp.dma_start(x_row0[:, :, b, :], src[b][:, :, 0:W]).then_inc(s_row0, 16)

                def load_half(c, h):
                    for b in range(B):
                        sp.dma_start(x_half[h][:, :, b, :], src[b][:, :, bass.ds(c * NPX + W + h * HPX, HPX)]).then_inc(s_load[h], 16)

                def load_residual(c, quarter):
                    h, b = quarter // 2, quarter % 2
                    sp.dma_start(res[quarter][:, :, :], px[b][:, bass.ds(c * PT + h * QT, QT), :]).then_inc(s_res[quarter], 16)

                def store(c, quarter):
                    h, b = quarter // 2, quarter % 2
                    sp.wait_ge(s_x1, MU * c + QM * (quarter + 1))
                    sp.dma_start(dst[b][:, bass.ds(c * PT + h * QT, QT), :], res[quarter][:, :, :]).then_inc(s_store[quarter], 16)

                def reload(c, quarter):
                    sp.wait_ge(s_store[quarter], 16 * c)
                    sp.wait_ge(s_st, MU * (c - 1) + QM * (quarter + 1))
                    load_residual(c, quarter)

                for h in range(2):
                    load_half(0, h)
                for quarter in range(4):
                    load_residual(0, quarter)
                for h in range(2):
                    sp.wait_ge(s_y, 4 + NU // 2 * (h + 1))
                    load_half(1, h)

                def body(i, first, last):
                    for s in range(2):
                        c = 2 * i + s
                        has_prev = not (first and s == 0)
                        for h in range(2):
                            if has_prev:
                                store(c - 1, 2 * h)
                                if h == 1:
                                    reload(c, 1)
                                store(c - 1, 2 * h + 1)
                                reload(c, 2 * h)
                            if not last:
                                sp.wait_ge(s_y, 4 + NU * (c + 1) + NU // 2 * (h + 1))
                                load_half(c + 2, h)
                        if has_prev:
                            reload(c, 3)
                loop(sp, NCH // 2, body)
                for quarter in range(4):
                    store(NCH - 1, quarter)
                for quarter in range(4):
                    sp.wait_ge(s_store[quarter], 16 * NCH)

            @block.gpsimd
            def _(pool):
                nc.gpsimd.memset(ones[:, :], 1.0).then_inc(s_one, 1)
                for j in range(3):
                    nc.gpsimd.memset(y[0][j][:, 0, :], 0.0).then_inc(s_edge, 1)

                pool.wait_ge(s_yev, 4 + NU * NCH)
                for j in range(3):
                    nc.gpsimd.memset(y[1][j][:, R + 1, :], 0.0).then_inc(s_edge, 1)

            @block.tensor
            def _(pe):
                def project(j, dst, xt, px0, n):
                    if j < 2:
                        for k in range(2):
                            ins = nc.tensor.matmul(dst[:, 0:n], wfold[j][:, k, 384:512], xt[:, k, j, px0:px0 + n],
                                                   start=(k == 0), stop=(k == 1))
                    else:
                        for b in range(B):
                            for k in range(2):
                                ins = nc.tensor.matmul(dst[64 * b:64 * b + 64, 0:n], wfold[b][:, k, 512:576],
                                                       xt[:, k, b, px0:px0 + n], start=(k == 0), stop=(k == 1))
                    ins.then_inc(s_y, 1)

                def conv_unit(c, n):
                    pe.wait_ge(s_yev, NU * c + n + 4 - 1)
                    h, q, j = order[n]
                    project(j, y_ps[n % 2], x_half[h], q * 512, 512)

                def mix_unit(c, s, m, early):
                    quarter, b, px0, r = image_of(m)
                    if not (early and m < 4):
                        pe.wait_ge(s_x1, MU * c + m - 3)
                    for t in range(2):
                        px = slice(px0 + 128 * t, px0 + 128 * t + 128)
                        nc.tensor.matmul(mix_ps[m % 4][:, C * t:C * t + C], acc[s][b][:, px], mix_a[b][:, :], start=True, stop=False,
                                         skip_group_check=True)
                        ins = nc.tensor.matmul(mix_ps[m % 4][:, C * t:C * t + C], acc[s][2][:, px], mix_c[b][:, :], start=False,
                                               stop=True, skip_group_check=True)
                    ins.then_inc(s_mix, 1)

                def stat_unit(c, s, m):
                    quarter, b, px0, r = image_of(m)
                    pe.wait_ge(s_sq, MU * c + m + 1)
                    for t in range(2):
                        for k in range(2):
                            col = 2 * k + b
                            ins = nc.tensor.matmul(st_ps[s][0:KC, col:col + 1], sq[m % 4][:, t, KC * k:KC * k + KC], ones[:, :],
                                                   start=(m == 0 and t == 0 and k == 0),
                                                   stop=(m == MU - 1 and t == 1 and k == 1), skip_group_check=True)
                    ins.then_inc(s_st, 1)

                def mix_begin(c, early):
                    pe.wait_ge(s_dw, 3 * NT * (c + 1))
                    if not early:
                        pe.wait_ge(s_sadd, c)

                def mix_step(c, s, m, early):
                    mix_unit(c, s, m, early)
                    if m >= 4:
                        stat_unit(c, s, m - 4)

                pe.wait_ge(s_row0, 32)
                for n in range(4):
                    if n >= 2:
                        pe.wait_ge(s_yev, n - 1)
                    project(n % 3, y_ps[n % 2], x_row0, 0, W)
                pe.wait_ge(s_one, 1)
                for n in range(NU):
                    if n == 0 or n == NU // 2:
                        pe.wait_ge(s_load[n // (NU // 2)], 32)
                    conv_unit(0, n)

                def body(i, first, last):
                    for s in range(2):
                        c = 2 * i + s
                        has_next = not (last and s == 1)
                        has_prev = not (first and s == 0)
                        if has_prev:
                            mix_begin(c - 1, first)
                        for n in range(NU):
                            if has_next:
                                if n == 0 or n == NU // 2:
                                    pe.wait_ge(s_load[n // (NU // 2)], 32 * (c + 2))
                                conv_unit(c + 1, n)
                            if has_prev:
                                for m in mix_after[n]:
                                    mix_step(c - 1, 1 - s, m, first and s == 1)
                        if has_prev:
                            for m in range(MU - 4, MU):
                                stat_unit(c - 1, 1 - s, m)
                loop(pe, NCH // 2, body)
                mix_begin(NCH - 1, False)
                for m in range(MU):
                    mix_step(NCH - 1, 1, m, False)
                for m in range(MU - 4, MU):
                    stat_unit(NCH - 1, 1, m)

            @block.scalar
            def _(act):
                def bias(j):
                    return bias_y[:, 3, j:j + 1] if j < 2 else bias_yc[:, :]

                def taps(j):
                    return 3 if j < 2 else 4

                def evict_y(c, s, n):
                    h, q, j = order[n]
                    r0 = 2 + (h * HU + q) * UR
                    act.wait_ge(s_y, 4 + NU * c + n + 1)
                    nc.scalar.activation(y[s][j][:, r0:r0 + UR, 1:W + 1], y_ps[n % 2][:, :].rearrange("p (r w) -> p r w", w=W),
                                         ACT.Identity, bias=bias(j)).then_inc(s_yev, 1)

                def square(c, m, early):
                    quarter, b, px0, r = image_of(m)
                    act.wait_ge(s_x1, MU * c + m + 1)
                    if m >= 4 or not early:
                        act.wait_ge(s_st, MU * c + m - 3)
                    nc.scalar.activation(sq[m % 4][:, :, :], res[quarter][:, 2 * r:2 * r + 2, :], ACT.Square).then_inc(s_sq, 1)

                for n in range(4):
                    act.wait_ge(s_y, n + 1)
                    nc.scalar.activation(y[0][n % 3][:, 1, 1:W + 1], y_ps[n % 2][:, 0:W], ACT.Identity, bias=bias(n % 3)).then_inc(s_yev, 1)
                for n in range(NU):
                    evict_y(0, 0, n)

                def body(i, first, last):
                    for s in range(2):
                        c = 2 * i + s
                        has_next = not (last and s == 1)
                        has_prev = not (first and s == 0)
                        if not first:
                            act.wait_ge(s_mix, MU * (c - 1))
                        act.wait_ge(s_edge, 3 * (c + 1) + (0 if has_next else 3))
                        act.wait_ge(s_yev, 4 + NU * (c + 1))
                        for j in range(3):
                            nc.scalar.activation(acc[s][j][:, :].rearrange("p (r w) -> p r w", w=W), y[s][j][:, 0:R, 0:W],
                                                 ACT.Identity, scale=v128[:, taps(j), VEC_TAP:VEC_TAP + 1],
                                                 bias=v128[:, taps(j), VEC_BDW:VEC_BDW + 1]).then_inc(s_acc, 1)
                        if has_next and has_prev:
                            act.wait_ge(s_dw, 3 * NT * c)
                        if has_next:
                            for j in range(3):
                                nc.scalar.activation(y[1 - s][j][:, 0:2, 1:W + 1], y[s][j][:, R:R + 2, 1:W + 1], ACT.Copy).then_inc(s_edge, 1)
                        for n in range(NU):
                            if has_next:
                                evict_y(c + 1, 1 - s, n)
                            if has_prev:
                                for m in mix_after[n]:
                                    square(c - 1, m, first and s == 1)
                loop(act, NCH // 2, body)
                for m in range(MU):
                    square(NCH - 1, m, False)

            @block.vector
            def _(dve):
                nc.vector.memset(x1_sq[:, :], 0.0).then_inc(s_sadd, 1)

                def add_residual(c, m):
                    quarter, b, px0, r = image_of(m)
                    dve.wait_ge(s_mix, MU * c + m + 1)
                    if r == 0:
                        dve.wait_ge(s_res[quarter], 16 * (c + 1))
                    x = res[quarter][:, 2 * r:2 * r + 2, :]
                    nc.vector.tensor_tensor(x, mix_ps[m % 4][:, 0:2 * C].rearrange("p (t c) -> p t c", t=2), x, ALU.add).then_inc(s_x1, 1)

                def add_sums(c, s):
                    dve.wait_ge(s_st, MU * (c + 1))
                    dve.wait_ge(s_sadd, c + 1)
                    nc.vector.tensor_tensor(x1_sq[:, :], st_ps[s][0:KC, 0:4], x1_sq[:, :], ALU.add).then_inc(s_sadd, 1)

                steps = 3 * NT
                mix_at = [[m for m in range(MU) if 6 + m * (steps - 7) // MU == n] for n in range(steps)]

                def body(i, first, last):
                    for s in range(2):
                        c = 2 * i + s
                        has_prev = not (first and s == 0)
                        for n, (dy, dx) in enumerate(V_TAPS):
                            for j in range(3):
                                if n == 0:
                                    dve.wait_ge(s_acc, 3 * c + j + 1)
                                else:
                                    dve.wait_ge(s_dw, 3 * NT * c + 3 * (n - 1) + j + 1)
                                tap = VEC_TAP + 3 * dy + dx
                                a = acc[s][j][:, :].rearrange("p (r w) -> p r w", w=W)
                                total = v_sums[:, j, bass.ds(c, 1)] if n == NT - 1 else None
                                nc.vector.scalar_tensor_tensor(a, y[s][j][:, dy:dy + R, dx:dx + W],
                                                               v128[:, 3 if j < 2 else 4, tap:tap + 1], a,
                                                               ALU.mult, ALU.add, accum_out=total).then_inc(s_dw, 1)
                                if has_prev:
                                    for m in mix_at[3 * n + j]:
                                        add_residual(c - 1, m)
                            if n == 0 and not first:
                                add_sums(c - 2, s)
                loop(dve, NCH // 2, body)
                add_sums(NCH - 2, 0)
                for m in range(MU):
                    add_residual(NCH - 1, m)
                add_sums(NCH - 1, 1)
                dve.wait_ge(s_sadd, NCH + 1)

        s_total, s_vmean, s_mean = sem("v_total"), sem("v_mixed_mean"), sem("v_mean")
        with nc.Block() as block:
            @block.tensor
            def _(pe):
                pe.wait_ge(s_total, 1)
                for k in range(2):
                    for b in range(B):
                        half = slice(KC * k, KC * k + KC)
                        col = slice(2 * k + b, 2 * k + b + 1)
                        nc.tensor.matmul(st_ps[0][0:KC, col], mix_a[b][:, half], v_total[:, b:b + 1], start=True, stop=False,
                                         skip_group_check=True)
                        ins = nc.tensor.matmul(st_ps[0][0:KC, col], mix_c[b][:, half], v_total[:, 2:3], start=False, stop=True,
                                               skip_group_check=True)
                ins.then_inc(s_vmean, 1)

            @block.vector
            def _(dve):
                nc.vector.tensor_reduce(v_total[:, :], v_sums[:, :, :], AX.X, ALU.add).then_inc(s_total, 1)
                dve.wait_ge(s_vmean, 1)
                nc.vector.scalar_tensor_tensor(x1_mean[:, :], st_ps[0][0:KC, 0:4], 1.0 / (H * W), moments[:, :, 0],
                                               ALU.mult, ALU.add).then_inc(s_mean, 1)
                dve.wait_ge(s_mean, 1)


def scan_coefficients(nc, sb, pb, sem, *, H, W, x1_sq, x1_mean, v96, gavg, scale, shift, gn_tmp, moments, co):
    s_mom, s_dve = sem("p2_mom"), sem("p2_dve")
    gn_sems = [sem(f"p2_gn{i}") for i in range(4)]
    inv = 1.0 / (H * W)
    with ExitStack() as ctx:
        ps = pb(ctx, "p2_ps", [128, 16])
        with nc.Block() as block:
            @block.vector
            def _(dve):
                n = [0]

                def link(ins):
                    n[0] += 1
                    ins.then_inc(s_dve, 1)
                    dve.wait_ge(s_dve, n[0])
                for k in range(2):
                    for b in range(B):
                        a = 2 * k + b
                        bo = v96[:, k, V_BOUT:V_BOUT + 1]
                        m, q = moments[:, a, 0:1], moments[:, a, 1:2]
                        t = gn_tmp[:, a:a + 1]
                        link(nc.vector.tensor_copy(m, x1_mean[:, a:a + 1]))
                        link(nc.vector.tensor_scalar(q, x1_sq[:, a:a + 1], inv, None, ALU.mult))
                        link(nc.vector.scalar_tensor_tensor(t, m, 2.0, bo, ALU.mult, ALU.add))
                        link(nc.vector.scalar_tensor_tensor(q, t, bo, q, ALU.mult, ALU.add))
                        link(nc.vector.tensor_tensor(m, m, bo, ALU.add))
                nc.vector.tensor_copy(gn_tmp[:, 0:1], moments[:, 0, 0:1]).then_inc(s_mom, 1)

        with nc.Block() as block:
            group_norm_scale(nc, block, moments, (s_mom, 1), ps, gn_tmp, scale, shift, gavg, 1e-5, gn_sems)

        s_co = sem("p2_co")
        with nc.Block() as block:
            @block.vector
            def _(dve):
                n = [0]

                def link(ins):
                    n[0] += 1
                    ins.then_inc(s_co, 1)
                    dve.wait_ge(s_co, n[0])
                for k in range(2):
                    for b in range(B):
                        def col(t):
                            return t[:, 2 * k + b:2 * k + b + 1]
                        bo, bv = v96[:, k, V_BOUT:V_BOUT + 1], v96[:, k, V_BV:V_BV + 1]
                        link(nc.vector.scalar_tensor_tensor(col(co["c_base"]), col(scale), bo, col(shift), ALU.mult, ALU.add))
                        link(nc.vector.tensor_scalar(col(co["c_tmp"]), v96[:, k, V_DV:V_DV + 1], v96[:, k, V_RES:V_RES + 1], None, ALU.add))
                        link(nc.vector.tensor_tensor(col(co["u_mul"]), col(scale), bv, ALU.mult))
                        link(nc.vector.tensor_tensor(col(co["u_add"]), col(co["c_base"]), bv, ALU.mult))
                        link(nc.vector.tensor_tensor(col(co["d_mul"]), col(scale), col(co["c_tmp"]), ALU.mult))
                        link(nc.vector.tensor_tensor(col(co["d_add"]), col(co["c_base"]), col(co["c_tmp"]), ALU.mult))
                        link(nc.vector.tensor_scalar(col(co["e_mul"]), col(co["d_mul"]), 2.0, 1.0, ALU.mult, ALU.add))
                        link(nc.vector.scalar_tensor_tensor(col(co["e_add"]), col(co["d_add"]), 2.0, bo, ALU.mult, ALU.add))


T = 8


def scan_phase(nc, sb, pb, sem, loop, *, along_w, H, W, HT, x1_d, part_d, out, amat, v96, co, ident):
    N = W if along_w else W + 2
    p = "w_" if along_w else "h_"
    G = 4
    PAIRS = T // 2
    s_zero = sem(p + "zero")
    s_load = [[sem(f"{p}load{b}{s}") for s in range(2)] for b in range(B)]
    s_part = [[sem(f"{p}part{b}{s}") for s in range(2)] for b in range(B)]
    s_store = [[sem(f"{p}store{b}{s}") for s in range(2)] for b in range(B)]
    s_xt = [sem(f"{p}x_transposed{b}") for b in range(B)]
    s_u = [sem(f"{p}u_ready{b}") for b in range(B)]
    s_mm = [sem(f"{p}products{b}") for b in range(B)]
    s_h = [sem(f"{p}state{b}") for b in range(B)]
    s_z = [sem(f"{p}z{b}") for b in range(B)]
    s_zt = [sem(f"{p}z_transposed{b}") for b in range(B)]
    s_out = [sem(f"{p}out{b}") for b in range(B)]
    s_dcol = [sem(f"{p}diag_in{b}") for b in range(B)]
    s_dz = [sem(f"{p}diag_out{b}") for b in range(B)]
    s_dload, s_dxt, s_dev = sem(p + "diag_load"), sem(p + "diag_transposed"), sem(p + "diag_evicted")

    def tile_of(t, k, tt, h):
        ch = slice(0, C) if k is None else slice(KC * k, KC * k + KC)
        return t[:, h, tt, ch] if along_w else t[:, tt, h, ch]

    with ExitStack() as ctx:
        gshape = [128, HT, G, C] if along_w else [128, G, HT, C]
        xs = [[sb(ctx, f"{p}x{b}{s}", gshape) for s in range(2)] for b in range(B)]
        os = [[sb(ctx, f"{p}o{b}{s}", gshape) for s in range(2)] for b in range(B)]
        us = [sb(ctx, f"{p}u{b}", [KC, 2, T, N]) for b in range(B)]
        zs = [sb(ctx, f"{p}z{b}", [KC, 2, T, W]) for b in range(B)]
        u = [[us[b][:, :, 2 * q:2 * q + 2, :] for q in range(PAIRS)] for b in range(B)]
        z = [[zs[b][:, :, 2 * q:2 * q + 2, :] for q in range(PAIRS)] for b in range(B)]
        hs = [sb(ctx, f"{p}h{b}", [KC, 2, T, N]) for b in range(B)]
        if not along_w:
            u_diag = [sb(ctx, f"u_diag{b}", [KC, 2, H, 2]) for b in range(B)]
            e_diag = [sb(ctx, f"e_diag{b}", [KC, 2, H, 2]) for b in range(B)]
            z_diag = [sb(ctx, f"z_diag{b}", [KC, 2, H, 2]) for b in range(B)]
            px_diag = sb(ctx, "px_diag", [128, B, 2, HT, C])
        h_ps = [pb(ctx, f"{p}h_ps{b}", [128, 2, 512]) for b in range(B)]
        x_ps = [pb(ctx, f"{p}x_ps{b}", [128, 512]) for b in range(B)]
        o_ps = [pb(ctx, f"{p}o_ps{b}", [128, 512]) for b in range(B)]

        def by_group(d, b):
            if along_w:
                return d[b].rearrange("(h p w) c -> p h w c", p=128, w=W)
            return d[b].rearrange("(y h p) c -> p y h c", p=128, h=HT)

        def group(view, n):
            return view[:, :, bass.ds(n * G, G), :] if along_w else view[:, bass.ds(n * G, G), :, :]

        def diagonal(d, b, which, h):
            step = W + 1 if which == 0 else W - 1
            start = (0 if which == 0 else W - 1) + 128 * h * step
            return d[b][start:start + 127 * step + 1:step, :]

        if not along_w:
            with nc.Block() as block:
                @block.sync
                def _(sp):
                    for b in range(B):
                        for d in range(2):
                            for h in range(HT):
                                sp.dma_start(px_diag[:, b, d, h, :], diagonal(x1_d, b, d, h)).then_inc(s_dload, 16)

                @block.tensor
                def _(pe):
                    pe.wait_ge(s_dload, 16 * B * 2 * HT)
                    for b in range(B):
                        for d in range(2):
                            n = 2 * b + d
                            if n >= 2:
                                pe.wait_ge(s_dev, 4 * (n - 1))
                            for k in range(2):
                                for h in range(HT):
                                    ins = nc.tensor.transpose(x_ps[d][0:KC, (HT * k + h) * 128:(HT * k + h) * 128 + 128],
                                                              px_diag[:, b, d, h, KC * k:KC * k + KC], ident)
                            ins.then_inc(s_dxt, 1)

                @block.scalar
                def _(act):
                    for b in range(B):
                        for d in range(2):
                            act.wait_ge(s_dxt, 2 * b + d + 1)
                            for k in range(2):
                                c = 2 * k + b
                                src = x_ps[d][0:KC, k * H:k * H + H]
                                nc.scalar.activation(u_diag[b][:, k, :, d], src, ACT.Identity, scale=co["u_mul"][:, c:c + 1],
                                                     bias=co["u_add"][:, c:c + 1]).then_inc(s_dev, 1)
                                nc.scalar.activation(e_diag[b][:, k, :, d], src, ACT.Identity, scale=co["d_mul"][:, c:c + 1],
                                                     bias=co["d_add"][:, c:c + 1]).then_inc(s_dev, 1)

        with nc.Block() as block:
            @block.sync
            def _(sp):
                xv = [by_group(x1_d, b) for b in range(B)]
                pv = [by_group(part_d, b) for b in range(B)]

                def load_x(n, s, wait):
                    for b in range(B):
                        if wait:
                            sp.wait_ge(s_xt[b], 4 * (n - 1))
                        sp.dma_start(xs[b][s][:, :, :, :], group(xv[b], n)).then_inc(s_load[b][s], 16)

                def load_part(n, i, s, wait):
                    for b in range(B):
                        if wait:
                            sp.wait_ge(s_store[b][s], 16 * i)
                        sp.dma_start(os[b][s][:, :, :, :], group(pv[b], n)).then_inc(s_part[b][s], 16)

                load_x(0, 0, False)

                def body(i, first, last):
                    for s in range(2):
                        if not (last and s == 1):
                            load_x(2 * i + s + 1, 1 - s, not (first and s == 0))
                        if along_w:
                            load_part(2 * i + s, i, s, not first)
                loop(sp, H // T, body)

            @block.gpsimd
            def _(pool):
                ov = [by_group(out if along_w else part_d, b) for b in range(B)]
                for b in range(B):
                    nc.gpsimd.memset(hs[b][:, :, T - 1, :], 0.0).then_inc(s_zero, 1)

                def store(n, s):
                    for b in range(B):
                        pool.wait_ge(s_out[b], G * (n + 1))
                        pool.dma_start(group(ov[b], n), os[b][s][:, :, :, :]).then_inc(s_store[b][s], 16)

                def body(i, first, last):
                    store(2 * i, 0)
                    store(2 * i + 1, 1)
                loop(pool, H // T, body)
                for b in range(B):
                    for s in range(2):
                        pool.wait_ge(s_store[b][s], 16 * (H // T))

            @block.tensor
            def _(pe):
                def transpose_x(i, b, P, k, wait_bank):
                    unit = 2 * (PAIRS * i + P) + k
                    if k == 0 and P % 2 == 0:
                        pe.wait_ge(s_load[b][(P // 2) % 2], 16 * (i + P // PAIRS + 1))
                    if wait_bank:
                        pe.wait_ge(s_u[b], unit)
                    for tt in range(2):
                        for h in range(HT):
                            col = (tt * HT + h) * 128
                            ins = nc.tensor.transpose(x_ps[b][0:KC, col:col + 128],
                                                      tile_of(xs[b][(P // 2) % 2], k, 2 * (P % 2) + tt, h), ident)
                    ins.then_inc(s_xt[b], 1)

                def transpose_z(i, b, t):
                    q = (t // 2) % PAIRS
                    if t % 2 == 0:
                        pe.wait_ge(s_z[b], T * i + t + 2)
                    pe.wait_ge(s_out[b], T * i + t) if not (isinstance(i, int) and T * i + t <= 0) else None
                    for h in range(HT):
                        for k in range(2):
                            ins = nc.tensor.transpose(o_ps[b][:, C * h + KC * k:C * h + KC * k + KC],
                                                      z[b][q][:, k, t % 2, 128 * h:128 * h + 128], ident[0:KC, 0:KC])
                    ins.then_inc(s_zt[b], 1)

                for b in range(B):
                    for k in range(2):
                        transpose_x(0, b, 0, k, k > 0)
                pe.wait_ge(s_zero, 2)

                def body(i, first, last):
                    for t in range(T):
                        for b in range(B):
                            if not (first and t == 0):
                                pe.wait_ge(s_h[b], T * i + t)
                            for j in range(2):
                                for k in range(2):
                                    ins = nc.tensor.matmul(h_ps[b][0:KC, j, 0:N], amat[:, k, KC * j:KC * j + KC],
                                                           hs[b][:, k, (t - 1) % T, :], start=(k == 0), stop=(k == 1))
                            ins.then_inc(s_mm[b], 1)
                            if not (last and t >= T - 2):
                                transpose_x(i, b, t // 2 + 1, t % 2, True)
                            if not (first and t < 3):
                                transpose_z(i, b, t - 3)
                loop(pe, H // T, body)
                for t in range(T - 3, T):
                    for b in range(B):
                        transpose_z(H // T - 1, b, t)

            @block.scalar
            def _(act):
                def make_u(i, b, P, k):
                    unit = 2 * (PAIRS * i + P) + k
                    q = P % PAIRS
                    c = 2 * k + b
                    act.wait_ge(s_xt[b], unit + 1)
                    if not (isinstance(i, int) and PAIRS * i + P < PAIRS):
                        act.wait_ge(s_h[b], 2 * (PAIRS * i + P - PAIRS) + 2)
                        if along_w:
                            act.wait_ge(s_zt[b], 2 * (PAIRS * i + P - PAIRS) + 2)
                    src = x_ps[b][0:KC, 0:2 * W].rearrange("p (t n) -> p t n", t=2)
                    ins = nc.scalar.activation(u[b][q][:, k, :, 0:W], src, ACT.Identity, scale=co["u_mul"][:, c:c + 1],
                                               bias=co["u_add"][:, c:c + 1])
                    if along_w:
                        ins = nc.scalar.activation(z[b][q][:, k, :, 0:W], src, ACT.Identity, scale=co["e_mul"][:, c:c + 1],
                                                   bias=co["e_add"][:, c:c + 1])
                    ins.then_inc(s_u[b], 1)

                def evict_out(i, b, t):
                    slot = (t // G) % 2
                    act.wait_ge(s_zt[b], T * i + t + 1)
                    if t % G == 0 and not (isinstance(i, int) and T * i + t < T):
                        act.wait_ge(s_store[b][slot], 16 * (i if t >= 0 else i - 1))
                    dst = os[b][slot][:, t % G, :, :]
                    nc.scalar.activation(dst, o_ps[b][:, 0:HT * C].rearrange("p (h c) -> p h c", c=C), ACT.Copy).then_inc(s_out[b], 1)

                for b in range(B):
                    for k in range(2):
                        make_u(0, b, 0, k)

                def body(i, first, last):
                    for t in range(T):
                        for b in range(B):
                            if not (last and t >= T - 2):
                                make_u(i, b, t // 2 + 1, t % 2)
                            if not along_w and not (first and t < 3):
                                evict_out(i, b, t - 3)
                loop(act, H // T, body)
                if not along_w:
                    for t in range(T - 3, T):
                        for b in range(B):
                            evict_out(H // T - 1, b, t)

            @block.vector
            def _(dve):
                def step_state(i, b, t, first):
                    q = t // 2
                    dve.wait_ge(s_mm[b], T * i + t + 1)
                    if t % 2 == 0:
                        dve.wait_ge(s_u[b], 2 * PAIRS * i + 2 * q + 2)
                        if not along_w:
                            dve.wait_ge(s_dcol[b], i + 1)
                            if t == 0 and not first:
                                dve.wait_ge(s_dz[b], 2 * i)
                        if not first:
                            dve.wait_ge(s_z[b], 2 * (PAIRS * i + q - PAIRS) + 2)
                    nc.vector.tensor_tensor(hs[b][:, :, t, :], h_ps[b][0:KC, :, 0:N], u[b][q][:, :, t % 2, :], ALU.add).then_inc(s_h[b], 1)

                def make_z(i, b, P, k, early):
                    q = P % PAIRS
                    dve.wait_ge(s_h[b], 2 * (PAIRS * i + P) + 2)
                    cv = v96[:, k, V_CV:V_CV + 1]
                    src = hs[b][:, k, 2 * q:2 * q + 2, 0:W]
                    dst = z[b][q][:, k, :, :]
                    if along_w:
                        nc.vector.scalar_tensor_tensor(dst, src, cv, dst, ALU.mult, ALU.add).then_inc(s_z[b], 1)
                    else:
                        if not early and k == 0:
                            dve.wait_ge(s_zt[b], 2 * (PAIRS * i + P - PAIRS) + 2)
                        nc.vector.tensor_scalar(dst, src, cv, None, ALU.mult).then_inc(s_z[b], 1)

                def add_part(i, b, t):
                    slot = (t // G) % 2
                    dve.wait_ge(s_zt[b], T * i + t + 1)
                    if t % G == 0:
                        dve.wait_ge(s_part[b][slot], 16 * (i + (1 if t >= 0 else 0)))
                    dst = os[b][slot][:, :, t % G, :]
                    nc.vector.tensor_tensor(dst, o_ps[b][:, 0:HT * C].rearrange("p (h c) -> p h c", c=C), dst, ALU.add).then_inc(s_out[b], 1)

                def diag_in(i, b):
                    nc.vector.tensor_scalar(us[b][:, :, :, W:W + 2], u_diag[b][:, :, bass.ds(T * i, T), :], 1.0, None, ALU.mult).then_inc(s_dcol[b], 1)

                def diag_out(i, b):
                    dve.wait_ge(s_h[b], T * (i + 1))
                    for k in range(2):
                        nc.vector.tensor_scalar(z_diag[b][:, k, bass.ds(T * i, T), :], hs[b][:, k, :, W:W + 2], v96[:, k, V_CV:V_CV + 1],
                                                None, ALU.mult).then_inc(s_dz[b], 1)

                if not along_w:
                    for b in range(B):
                        diag_in(0, b)

                def body(i, first, last):
                    for t in range(T):
                        for b in range(B):
                            step_state(i, b, t, first)
                            if along_w:
                                o, to = (1, t - 4) if b == 0 else (0, t - 3)
                                if not (first and to < 0):
                                    add_part(i, o, to)
                            if t % 2 == 1:
                                make_z(i, b, t // 2, 0, first)
                            elif not (first and t == 0):
                                make_z(i, b, t // 2 - 1, 1, first)
                    if not along_w:
                        for b in range(B):
                            diag_out(i, b)
                            if not last:
                                diag_in(i + 1, b)
                loop(dve, H // T, body)
                last = H // T - 1
                for b in range(B):
                    make_z(last, b, PAIRS - 1, 1, False)
                if along_w:
                    add_part(last, 1, T - 4)
                    for t in range(T - 3, T):
                        for b in range(B):
                            add_part(last, b, t)

        if not along_w:
            s_fix = [sem("fix_" + n) for n in ("sum", "load", "zt", "add", "store")]
            s_sum, s_fload, s_fzt, s_add, s_fst = s_fix
            with nc.Block() as block:
                @block.sync
                def _(sp):
                    for b in range(B):
                        for d in range(2):
                            for h in range(HT):
                                sp.dma_start(px_diag[:, b, d, h, :], diagonal(part_d, b, d, h)).then_inc(s_fload, 16)
                    n = 0
                    for b in range(B):
                        for d in range(2):
                            n += 1
                            sp.wait_ge(s_add, n)
                            for h in range(HT):
                                sp.dma_start(diagonal(part_d, b, d, h), px_diag[:, b, d, h, :]).then_inc(s_fst, 16)
                    sp.wait_ge(s_fst, 16 * B * 2 * HT)

                @block.vector
                def _(dve):
                    for b in range(B):
                        nc.vector.tensor_tensor(z_diag[b][:, :, :, :], z_diag[b][:, :, :, :], e_diag[b][:, :, :, :], ALU.add).then_inc(s_sum, 1)
                    dve.wait_ge(s_fload, 16 * B * 2 * HT)
                    for b in range(B):
                        for d in range(2):
                            dve.wait_ge(s_fzt, 2 * b + d + 1)
                            dst = px_diag[:, b, d, :, :]
                            nc.vector.tensor_tensor(dst, x_ps[d][:, 0:HT * C].rearrange("p (h c) -> p h c", c=C), dst, ALU.add).then_inc(s_add, 1)

                @block.tensor
                def _(pe):
                    pe.wait_ge(s_sum, 2)
                    for b in range(B):
                        for d in range(2):
                            if b > 0:
                                pe.wait_ge(s_add, 2 * b + d - 1)
                            for h in range(HT):
                                for k in range(2):
                                    ins = nc.tensor.transpose(x_ps[d][:, C * h + KC * k:C * h + KC * k + KC],
                                                              z_diag[b][:, k, 128 * h:128 * h + 128, d], ident[0:KC, 0:KC])
                            ins.then_inc(s_fzt, 1)


def kernel(x, L0_conv_w_qkv, L0_conv_b_qkv, L0_conv_w_dw, L0_conv_b_dw, L0_conv_temperature, L0_conv_w_out, L0_conv_b_out,
           L1_conv_A, L1_conv_Bv, L1_conv_Cv, L1_conv_Dv, L1_conv_res_scale):
    import concourse.bacc as bacc
    from concourse.bass_utils import run_bass_kernel_spmd

    x = np.asarray(x)
    nb, H, W, nch = x.shape
    x_cm = np.zeros((B, C, H + 1, W), np.float32)
    x_cm[:, :, :H] = x.transpose(0, 3, 1, 2)

    w_dw, b_qkv, b_dw = (np.asarray(a) for a in (L0_conv_w_dw, L0_conv_b_qkv, L0_conv_b_dw))
    rows = np.concatenate([w_dw.reshape(9, 3 * C), b_qkv[None], b_dw[None]]).T
    last = rows[512:576]
    vec128 = np.stack([rows[0:128], rows[128:256], rows[256:384], rows[384:512], np.concatenate([last, last])], axis=1)

    temp = np.repeat(np.asarray(L0_conv_temperature).reshape(4), C // 4)
    res_scale = np.repeat(np.asarray(L1_conv_res_scale), C)
    cols = [L1_conv_Bv, L1_conv_Cv, L1_conv_Dv, L0_conv_b_out, temp, res_scale]
    vec96 = np.stack([np.asarray(c).reshape(2, KC) for c in cols], axis=-1).transpose(1, 0, 2)

    ch = np.arange(KC)
    select = np.eye(384, dtype=np.float32).reshape(3, 128, 384).transpose(1, 0, 2)
    gavg = ((ch[:, None] // GROUP) == (ch[None] // GROUP)).astype(np.float32) / np.float32(GROUP)
    mask = np.where((ch[:, None] // 48) == (ch[None] // 48), 0.0, -1e30).astype(np.float32)

    def halves(w):
        return np.asarray(w).reshape(2, KC, -1).transpose(1, 0, 2)

    inputs = dict(x_cm=x_cm.reshape(B, C, (H + 1) * W), x_px=x.reshape(B, H * W, C), w_qkv=halves(L0_conv_w_qkv), w_out=halves(L0_conv_w_out),
                  a_mat=halves(L1_conv_A), vec128=vec128, vec96=vec96, select=select, gavg_d=gavg, mask_d=mask)
    inputs = {k: np.ascontiguousarray(v) for k, v in inputs.items()}
    nc = bacc.Bacc("TRN2", target_bir_lowering=False, num_devices=1)
    aps = {k: nc.dram_tensor(k, list(v.shape), F32, kind="ExternalInput").ap() for k, v in inputs.items()}
    x1_d = nc.dram_tensor("x1_d", [B, H * W, C], F32, kind="Internal").ap()
    part_d = nc.dram_tensor("part_d", [B, H * W, C], F32, kind="Internal").ap()
    out = nc.dram_tensor("out", [B, H * W, C], F32, kind="ExternalOutput").ap()
    build(nc, **aps, x1_d=x1_d, part_d=part_d, out=out, H=H, W=W)
    r = run_bass_kernel_spmd(nc, [inputs], core_ids=[0])
    return r.results[0]["out"].reshape(B, H, W, C)
```

```python
import numpy as np
import concourse.bass as bass
from concourse import mybir
from contextlib import ExitStack

F32 = mybir.dt.float32
BF16 = mybir.dt.bfloat16
ALU = mybir.AluOpType
ACT = mybir.ActivationFunctionType
AX = mybir.AxisListType

C = 192
KC = 96
B = 2
R = 8
GROUP = 6
VEC_TAP, VEC_BQKV, VEC_BDW = 0, 9, 10
V_BV, V_CV, V_DV, V_BOUT, V_RES = range(5)
V_TEMP = 5
PSUM_BANK = 512


def group_norm_scale(nc, block, raw, mean_sq_ready, group_sum, tmp, scale, shift, gavg, eps, sems):
    s_avg, s_var, s_std, s_done = sems

    @block.tensor
    def _(pe):
        pe.wait_ge(mean_sq_ready[0], mean_sq_ready[1])
        nc.tensor.matmul(group_sum[0:KC, 0:8], gavg[:, :], raw[:, :, :], start=True, stop=True).then_inc(s_avg, 1)

    @block.vector
    def _(dve):
        dve.wait_ge(s_avg, 1)
        g = group_sum[0:KC, 0:8].rearrange("p (a m) -> p a m", m=2)
        nc.vector.tensor_copy(tmp[:, 0:4], g[:, :, 0]).then_inc(s_done, 1)
        dve.wait_ge(s_done, 1)
        nc.vector.tensor_tensor(tmp[:, 4:8], tmp[:, 0:4], tmp[:, 0:4], ALU.mult).then_inc(s_done, 1)
        dve.wait_ge(s_done, 2)
        nc.vector.tensor_tensor(tmp[:, 8:12], g[:, :, 1], tmp[:, 4:8], ALU.subtract).then_inc(s_done, 1)
        dve.wait_ge(s_done, 3)
        nc.vector.tensor_scalar_add(tmp[:, 12:16], tmp[:, 8:12], eps).then_inc(s_var, 1)
        dve.wait_ge(s_std, 1)
        nc.vector.reciprocal(scale[:, :], tmp[:, 16:20]).then_inc(s_done, 1)
        dve.wait_ge(s_done, 4)
        nc.vector.scalar_tensor_tensor(shift[:, :], tmp[:, 0:4], -1.0, scale[:, :], ALU.mult, ALU.mult).then_inc(s_done, 1)
        dve.wait_ge(s_done, 5)

    @block.scalar
    def _(act):
        act.wait_ge(s_var, 1)
        nc.scalar.activation(tmp[:, 16:20], tmp[:, 12:16], ACT.Sqrt).then_inc(s_std, 1)


def build(nc, x_cm, x_px, w_qkv, w_out, a_mat, vec128, vec96, vec_scan, select, gavg_d, mask_d, x1_d, part_d, out, H, W):
    NPX = R * W
    UNITS = NPX // PSUM_BANK
    UR = PSUM_BANK // W
    NCH = H // R
    PT = NPX // 128
    YW = W + 2
    HT = W // 128
    assert H == W and NCH % 2 == 0 and NCH >= 6

    outer = ExitStack()

    names = {}

    def unique(name):
        names[name] = names.get(name, 0) + 1
        return name if names[name] == 1 else f"{name}_{names[name]}"

    def sb(ctx, name, shape, dt=F32):
        return ctx.enter_context(nc.sbuf_tensor(unique(name), shape, dt))

    def pb(ctx, name, shape):
        return ctx.enter_context(nc.psum_tensor(unique(name), shape, F32))

    live = []

    def sem(name):
        live.append(nc.alloc_semaphore(name=unique("s_" + name)))
        return live[-1]

    def end_phase():
        nc.clear_and_free_semaphores(live)
        nc.all_engine_barrier()
        live.clear()

    def loop(eng, n, body):
        body(0, True, False)
        with eng.Fori(1, n - 1) as i:
            body(i, False, False)
        body(n - 1, False, True)

    with outer:
        sel = sb(outer, "sel", [128, 3, 384])
        gavg = sb(outer, "gavg", [KC, KC])
        mask = sb(outer, "mask", [KC, KC])
        v128 = sb(outer, "v128", [128, 5, 11])
        v96 = sb(outer, "v96", [KC, 2, 6])
        amat = sb(outer, "amat", [128, 4, 128])
        v_scan = sb(outer, "v_scan", [128, 3, 5])
        wout = sb(outer, "wout", [KC, 2, C])
        scale1 = sb(outer, "scale1", [KC, 4])
        shift1 = sb(outer, "shift1", [KC, 4])
        scale2 = sb(outer, "scale2", [KC, 4])
        shift2 = sb(outer, "shift2", [KC, 4])
        gn_tmp = sb(outer, "gn_tmp", [KC, 20])
        moments = sb(outer, "moments", [KC, 4, 2])
        ident = sel[:, 0, 0:128]
        x1_sq = sb(outer, "x1_sq", [KC, 4])
        x1_mean = sb(outer, "x1_mean", [KC, 4])

        with ExitStack() as conv:
            wraw = sb(conv, "wraw", [KC, 2, 3 * C])
            wfold = [sb(conv, f"wfold{b}", [KC, 2, 3 * C]) for b in range(B)]
            bias_y = sb(conv, "bias_y", [128, 4, 2])
            bias_yc = sb(conv, "bias_yc", [128, 1])
            x_in = [sb(conv, f"x_in{s}", [KC, 2, NPX]) for s in range(2)]
            y = [[sb(conv, f"y{s}_{j}", [128, R + 2, YW]) for j in range(3)] for s in range(2)]
            acc = [[sb(conv, f"acc{s}_{j}", [128, NPX]) for j in range(3)] for s in range(2)]
            mix_a = [sb(conv, f"mix_a{b}", [128, C]) for b in range(B)]
            mix_c = [sb(conv, f"mix_c{b}", [128, C]) for b in range(B)]

            stats_phase(nc, sb, pb, sem, loop, 
                NPX=NPX, UNITS=UNITS, NCH=NCH, x_cm=x_cm, x_in=x_in, acc=acc, y=y, sel=sel, gavg=gavg, mask=mask,
                v128=v128, v96=v96, v_scan=v_scan, amat=amat, wout=wout, wraw=wraw, wfold=wfold, bias_y=bias_y, bias_yc=bias_yc,
                scale=scale1, shift=shift1, gn_tmp=gn_tmp, moments=moments, w_qkv=w_qkv, w_out=w_out, a_mat=a_mat,
                vec128=vec128, vec96=vec96, vec_scan=vec_scan, select=select, gavg_d=gavg_d, mask_d=mask_d)
            end_phase()

            for b in range(B):
                with ExitStack() as qk:
                    gram = sb(qk, "gram", [KC, 2, KC])
                    sq_norm = sb(qk, "sq_norm", [128, 3, NCH])
                    qk_phase(nc, sb, pb, sem, loop, 
                        b=b, NPX=NPX, UNITS=UNITS, UR=UR, NCH=NCH, PT=PT, H=H, W=W, x_cm=x_cm, x_in=x_in, y=y, acc=acc,
                        wfold=wfold[b], bias_y=bias_y, v128=v128, ident=ident, gram=gram, sq_norm=sq_norm)
                    attention_phase(nc, sb, pb, sem, 
                        b=b, NCH=NCH, gram=gram, sq_norm=sq_norm, sel=sel, mask=mask, v96=v96, wout=wout,
                        mix_a=mix_a[b], mix_c=mix_c[b])
                    end_phase()

            v_phase(nc, sb, pb, sem, loop, 
                NPX=NPX, UNITS=UNITS, UR=UR, NCH=NCH, PT=PT, H=H, W=W, x_cm=x_cm, x_px=x_px, x1_d=x1_d, x_in=x_in,
                y=y, acc=acc, wfold=wfold, bias_y=bias_y, bias_yc=bias_yc, v128=v128, mix_a=mix_a, mix_c=mix_c,
                x1_sq=x1_sq, x1_mean=x1_mean, moments=moments, sel=sel)
            end_phase()

        with ExitStack() as scan:
            co = {n: sb(scan, n, [128, 3]) for n in ("u_mul", "u_add", "e_mul", "e_add", "d_mul", "d_add", "c_tmp", "c_base")}
            co["scale_shift"] = sb(scan, "scale_shift", [128, 3, 2])
            scan_coefficients(nc, sb, pb, sem, 
                H=H, W=W, x1_sq=x1_sq, x1_mean=x1_mean, v96=v96, v_scan=v_scan, sel=sel, gavg=gavg, scale=scale2, shift=shift2, gn_tmp=gn_tmp,
                moments=moments, co=co)
            for vertical in (False, True):
                scan_phase(nc, sb, pb, sem, loop, 
                    along_w=vertical, H=H, W=W, HT=HT, x1_d=x1_d, part_d=part_d, out=out, amat=amat, v_scan=v_scan, co=co, ident=ident)
                end_phase()


def stats_phase(nc, sb, pb, sem, loop, *, NPX, UNITS, NCH, x_cm, x_in, acc, y, sel, gavg, mask, v128, v96, v_scan,
                amat, wout, wraw, wfold, bias_y, bias_yc, scale, shift, gn_tmp, moments, w_qkv, w_out, a_mat, vec128, vec96, vec_scan,
                select, gavg_d, mask_d):
    s_const, s_side = sem("p1_const"), sem("p1_side")
    slots = [[x_in[s][:, k, :] for k in range(2)] for s in range(2)] + [[acc[s][k][0:KC, :] for k in range(2)] for s in range(2)]
    NS = len(slots)
    assert NCH % NS == 0
    s_load = [sem(f"p1_load{s}") for s in range(NS)]
    s_used, s_dve, s_mom = sem("p1_used"), sem("p1_dve"), sem("p1_mom")
    gn_sems = [sem(f"p1_gn{i}") for i in range(4)]
    with ExitStack() as ctx:
        stats = [sb(ctx, f"bn_stats{b}", [KC, 2, NCH * UNITS, 6]) for b in range(B)]
        mv = sb(ctx, "bn_mv", [KC, 4, 2])
        ps = pb(ctx, "p1_ps", [128, 16])
        with nc.Block() as block:
            @block.sync
            def _(sp):
                for dst, src in ((wraw, w_qkv), (wout, w_out), (amat, a_mat), (v128, vec128),
                                 (v96, vec96), (v_scan, vec_scan), (sel, select)):
                    sp.dma_start(dst[:, :, :], src).then_inc(s_const, 16)
                sp.dma_start(gavg[:, :], gavg_d).then_inc(s_const, 16)
                sp.dma_start(mask[:, :], mask_d).then_inc(s_const, 16)
                for b in range(B):
                    src = x_cm[b].rearrange("(k c) n -> c k n", k=2)

                    def body(i, first, last):
                        for s in range(NS):
                            if not (first and b == 0):
                                sp.wait_ge(s_used, b * NCH + NS * i + s - NS + 1)
                            for k in range(2):
                                sp.dma_start(slots[s][k], src[:, k, bass.ds((NS * i + s) * NPX, NPX)]).then_inc(s_load[s], 16)
                    loop(sp, NCH // NS, body)
                sp.wait_ge(s_const, 16 * 9)

            @block.gpsimd
            def _(pool):
                for s in range(2):
                    for j in range(3):
                        nc.gpsimd.memset(y[s][j][:, :, :], 0.0).then_inc(s_side, 1)
                pool.wait_ge(s_side, 6)

            @block.vector
            def _(dve):
                for b in range(B):
                    def body(i, first, last):
                        for s in range(NS):
                            dve.wait_ge(s_load[s], 32 * (b * (NCH // NS) + i + 1))
                            for k in range(2):
                                for u in range(UNITS):
                                    ins = nc.vector.bn_stats(
                                        stats[b][:, k, bass.ds((NS * i + s) * UNITS + u, 1), :].rearrange("p a c -> p (a c)"),
                                        slots[s][k][:, u * 512:(u + 1) * 512])
                            ins.then_inc(s_used, 1)
                    loop(dve, NCH // NS, body)
                dve.wait_ge(s_used, B * NCH)
                for b in range(B):
                    for k in range(2):
                        nc.vector.bn_aggr(mv[:, 2 * k + b, :], stats[b][:, k, :, :].rearrange("p a c -> p (a c)")).then_inc(s_dve, 1)
                dve.wait_ge(s_dve, 4)
                nc.vector.tensor_tensor(moments[:, :, 0], mv[:, :, 0], mv[:, :, 0], ALU.mult).then_inc(s_dve, 1)
                dve.wait_ge(s_dve, 5)
                nc.vector.tensor_tensor(moments[:, :, 1], mv[:, :, 1], moments[:, :, 0], ALU.add).then_inc(s_dve, 1)
                dve.wait_ge(s_dve, 6)
                nc.vector.tensor_copy(moments[:, :, 0], mv[:, :, 0]).then_inc(s_mom, 1)

        with nc.Block() as block:
            group_norm_scale(nc, block, moments, (s_mom, 1), ps, gn_tmp, scale, shift, gavg, 1e-5, gn_sems)

        s_bias, s_fold = sem("p1_bias"), sem("p1_fold")
        with nc.Block() as block:
            @block.tensor
            def _(pe):
                for j in range(4):
                    for k in range(2):
                        nc.tensor.matmul(ps[:, 2 * j:2 * j + 2], wraw[:, k, 128 * j:128 * j + 128], shift[:, 2 * k:2 * k + 2],
                                         start=(k == 0), stop=(k == 1))
                for b in range(B):
                    for k in range(2):
                        ins = nc.tensor.matmul(ps[64 * b:64 * b + 64, 8:9], wraw[:, k, 512:576], shift[:, 2 * k + b:2 * k + b + 1],
                                               start=(k == 0), stop=(k == 1))
                ins.then_inc(s_bias, 1)

            @block.vector
            def _(dve):
                for b in range(B):
                    for k in range(2):
                        nc.vector.tensor_scalar(wfold[b][:, k, :], wraw[:, k, :], scale[:, 2 * k + b:2 * k + b + 1], None,
                                                ALU.mult).then_inc(s_fold, 1)
                dve.wait_ge(s_bias, 1)
                for j in range(4):
                    nc.vector.tensor_scalar(bias_y[:, j, :], ps[:, 2 * j:2 * j + 2], v128[:, j, VEC_BQKV:VEC_BQKV + 1], None,
                                            ALU.add).then_inc(s_fold, 1)
                nc.vector.tensor_tensor(bias_yc[:, :], ps[:, 8:9], v128[:, 4, VEC_BQKV:VEC_BQKV + 1], ALU.add).then_inc(s_fold, 1)
                dve.wait_ge(s_fold, 9)


ALL_TAPS = tuple((dy, dx) for dy in range(3) for dx in range(3))
QK_PE_TAPS = (ALL_TAPS[:3], ALL_TAPS[:2], ())
V_PE_TAPS = (ALL_TAPS[:2], (), ())


def dve_order(pe_taps):
    mine = [ALL_TAPS[max(len(taps), 1):] for taps in pe_taps]
    rounds = max(len(taps) for taps in mine)
    ops = [(j, mine[j][n - rounds + len(mine[j])]) for n in range(rounds) for j in range(3) if n >= rounds - len(mine[j])]
    return [(j, tap, max((m for m in range(n) if ops[m][0] == j), default=None)) for n, (j, tap) in enumerate(ops)]


def qk_phase(nc, sb, pb, sem, loop, *, b, NPX, UNITS, UR, NCH, PT, H, W, x_cm, x_in, y, acc, wfold, bias_y, v128, ident,
             gram, sq_norm):
    NU = 3 * UNITS
    order = dve_order(QK_PE_TAPS)
    NDW = len(order)
    NTU = 2 * UNITS
    NA = NTU + 1
    pe_taps = [(j, tap) for j in range(3) for tap in QK_PE_TAPS[j]]
    p = f"qk{b}_"
    s_row0, s_diag = sem(p + "row0"), sem(p + "diag")
    s_load = [sem(f"{p}load{s}") for s in range(2)]
    s_y, s_yev = sem(p + "y_ready"), sem(p + "y_evicted")
    s_edge = sem(p + "edge_rows")
    s_tap, s_acc = sem(p + "taps_ready"), sem(p + "acc_started")
    s_dw = sem(p + "dw_ops")
    s_t, s_tev = sem(p + "transposed"), sem(p + "transposed_evicted")
    s_gram, s_gadd, s_sq = sem(p + "gram_tile"), sem(p + "gram_added"), sem(p + "squared")
    with ExitStack() as ctx:
        x_row0 = sb(ctx, "x_row0", [KC, 2, W])
        diag = sb(ctx, "diag", [128, len(pe_taps), 128])
        qk_t = [sb(ctx, f"qk_t{s}", [128, 384]) for s in range(4)]
        junk = sb(ctx, "junk", [128, NPX], BF16)
        y_ps = [pb(ctx, f"y_ps{s}", [128, 512]) for s in range(2)]
        tap_ps = [pb(ctx, f"tap_ps{s}", [128, 512]) for s in range(2)]
        t_ps = [pb(ctx, f"t_ps{s}", [128, 512]) for s in range(2)]
        gram_ps = [pb(ctx, f"gram_ps{s}", [128, 512]) for s in range(2)]
        tiles_after = [range(u * PT // NU, (u + 1) * PT // NU) for u in range(NU)]

        def yview(t, dy, dx, r0, rows):
            return t[:, dy + r0:dy + r0 + rows, dx:dx + W]

        with nc.Block() as block:
            @block.sync
            def _(sp):
                src = x_cm[b].rearrange("(k c) n -> c k n", k=2)
                sp.dma_start(x_row0[:, :, :], src[:, :, 0:W]).then_inc(s_row0, 16)

                def body(i, first, last):
                    for s in range(2):
                        if not first:
                            sp.wait_ge(s_y, 3 + NU * (2 * i + s - 1))
                        sp.dma_start(x_in[s][:, :, :], src[:, :, bass.ds((2 * i + s) * NPX + W, NPX)]).then_inc(s_load[s], 16)
                loop(sp, NCH // 2, body)

            @block.gpsimd
            def _(pool):
                for j in range(3):
                    nc.gpsimd.memset(y[0][j][:, 0, :], 0.0).then_inc(s_edge, 1)

                pool.wait_ge(s_yev, 3 + NU * NCH)
                for j in range(3):
                    nc.gpsimd.memset(y[1][j][:, R + 1, :], 0.0).then_inc(s_edge, 1)

            @block.tensor
            def _(pe):
                def project(j, u, dst, xt, n):
                    for k in range(2):
                        ins = nc.tensor.matmul(dst[:, 0:n], wfold[:, k, 128 * j:128 * j + 128],
                                               xt[:, k, u * 512:u * 512 + n], start=(k == 0), stop=(k == 1))
                    ins.then_inc(s_y, 1)

                def conv_unit(c, s, u, skip_wait):
                    if not skip_wait:
                        pe.wait_ge(s_yev, NU * c + u + 3 - 1)
                    project(u // UNITS, u % UNITS, y_ps[(u + 3) % 2], x_in[s], 512)

                def transpose_tile(c, s, t, skip_wait):
                    if not skip_wait:
                        pe.wait_ge(s_tev, PT * c + t - 1)
                    for j in range(3):
                        ins = nc.tensor.transpose(t_ps[t % 2][:, 128 * j:128 * j + 128], acc[s][j][:, 128 * t:128 * t + 128], ident)
                    ins.then_inc(s_t, 1)

                def gram_tile(c, s, t):
                    pe.wait_ge(s_tev, PT * c + t + 1)
                    for hp in range(2):
                        ins = nc.tensor.matmul(gram_ps[s][0:KC, KC * hp:KC * hp + KC], qk_t[t % 4][:, KC * hp:KC * hp + KC],
                                               qk_t[t % 4][:, C + KC * hp:C + KC * hp + KC], start=(t == 0 and hp == 0),
                                               stop=(t == PT - 1 and hp == 1), skip_group_check=True)
                    ins.then_inc(s_gram, 1)

                def gram_step(c, s, t, first):
                    transpose_tile(c, s, t, first and t < 2)
                    if t >= 2:
                        gram_tile(c, s, t - 2)

                def gram_begin(c, early):
                    pe.wait_ge(s_dw, NDW * (c + 1))
                    if not early:
                        pe.wait_ge(s_gadd, c)

                def taps(c, s, first):
                    for u in range(NTU):
                        j, q = 1 - u // UNITS, u % UNITS
                        if q == 0:
                            pe.wait_ge(s_yev, 3 + NU * c + UNITS * (j + 1))
                        if u == 0:
                            pe.wait_ge(s_edge, 3 * (c + 1))
                        if not (first and u < 2):
                            pe.wait_ge(s_acc, NA * c + (u if u >= 2 else u - 1))
                        for n, (dy, dx) in enumerate(QK_PE_TAPS[j]):
                            ins = nc.tensor.matmul(tap_ps[u % 2][:, :], diag[:, pe_taps.index((j, (dy, dx))), :],
                                                   yview(y[s][j], dy, dx, q * UR, UR), start=(n == 0), stop=(n == len(QK_PE_TAPS[j]) - 1))
                        ins.then_inc(s_tap, 1)

                pe.wait_ge(s_row0, 16)
                for j in range(3):
                    if j == 2:
                        pe.wait_ge(s_yev, 1)
                    project(j, 0, y_ps[j % 2], x_row0, W)
                pe.wait_ge(s_load[0], 16)
                for u in range(NU):
                    conv_unit(0, 0, u, False)
                pe.wait_ge(s_diag, len(pe_taps))
                taps(0, 0, True)

                def body(i, first, last):
                    for s in range(2):
                        c = 2 * i + s
                        has_next = not (last and s == 1)
                        has_prev = not (first and s == 0)
                        step(c, i, s, has_next, has_prev, first and s == 1, first)

                def step(c, i, s, has_next, has_prev, prev_first, early):
                    if has_next:
                        pe.wait_ge(s_load[1 - s], 16 * (i + 1 + s))
                    if has_prev:
                        gram_begin(c - 1, early)
                    for u in range(NU):
                        if has_next:
                            conv_unit(c + 1, 1 - s, u, False)
                        if has_prev:
                            for t in tiles_after[u]:
                                gram_step(c - 1, 1 - s, t, prev_first)
                    if has_prev:
                        for t in (PT - 2, PT - 1):
                            gram_tile(c - 1, 1 - s, t)
                    if has_next:
                        taps(c + 1, 1 - s, False)
                loop(pe, NCH // 2, body)
                gram_begin(NCH - 1, False)
                for t in range(PT):
                    gram_step(NCH - 1, 1, t, False)
                for t in (PT - 2, PT - 1):
                    gram_tile(NCH - 1, 1, t)

            @block.scalar
            def _(act):
                def evict_y(c, s, u):
                    j, q = u // UNITS, u % UNITS
                    act.wait_ge(s_y, 3 + NU * c + u + 1)
                    nc.scalar.activation(y[s][j][:, 2 + q * UR:2 + q * UR + UR, 1:W + 1],
                                         y_ps[(u + 3) % 2][:, :].rearrange("p (r w) -> p r w", w=W), ACT.Identity,
                                         bias=bias_y[:, j, b:b + 1]).then_inc(s_yev, 1)

                def evict_t(c, t, first_use):
                    act.wait_ge(s_t, PT * c + t + 1)
                    if not (first_use and t < 4):
                        act.wait_ge(s_gram, PT * c + t - 3)
                    nc.scalar.activation(qk_t[t % 4][:, :], t_ps[t % 2][:, 0:384], ACT.Copy).then_inc(s_tev, 1)

                def start_acc(c, s):
                    act.wait_ge(s_edge, 3 * (c + 1))
                    act.wait_ge(s_yev, 3 + NU * (c + 1))
                    nc.scalar.activation(acc[s][2][:, :].rearrange("p (r w) -> p r w", w=W), y[s][2][:, 0:R, 0:W],
                                         ACT.Identity, scale=v128[:, 2, VEC_TAP:VEC_TAP + 1],
                                         bias=v128[:, 2, VEC_BDW:VEC_BDW + 1]).then_inc(s_acc, 1)
                    for u in range(NTU):
                        j, q = 1 - u // UNITS, u % UNITS
                        act.wait_ge(s_tap, NTU * c + u + 1)
                        nc.scalar.activation(acc[s][j][:, q * 512:(q + 1) * 512], tap_ps[u % 2][:, :], ACT.Identity,
                                             bias=v128[:, j, VEC_BDW:VEC_BDW + 1]).then_inc(s_acc, 1)

                def squares(c, s, tiles=range(3)):
                    act.wait_ge(s_dw, NDW * (c + 1))
                    for j in tiles:
                        act.wait_ge(s_sq, 3 * c + j)
                        nc.scalar.activation(junk[:, :], acc[s][j][:, :], ACT.Square,
                                             accum_out=sq_norm[:, j, bass.ds(c, 1)]).then_inc(s_sq, 1)

                for j in range(3):
                    act.wait_ge(s_y, j + 1)
                    nc.scalar.activation(y[0][j][:, 1, 1:W + 1], y_ps[j % 2][:, 0:W], ACT.Identity,
                                         bias=bias_y[:, j, b:b + 1]).then_inc(s_yev, 1)
                for u in range(NU):
                    evict_y(0, 0, u)
                start_acc(0, 0)

                def body(i, first, last):
                    for s in range(2):
                        c = 2 * i + s
                        has_next = not (last and s == 1)
                        has_prev = not (first and s == 0)
                        if has_next:
                            if has_prev:
                                act.wait_ge(s_dw, NDW * c)
                            act.wait_ge(s_yev, 3 + NU * (c + 1))
                            for j in range(3):
                                nc.scalar.activation(y[1 - s][j][:, 0:2, 1:W + 1], y[s][j][:, R:R + 2, 1:W + 1], ACT.Copy).then_inc(s_edge, 1)
                        for u in range(NU):
                            if has_next:
                                evict_y(c + 1, 1 - s, u)
                            if has_prev:
                                for t in tiles_after[u]:
                                    evict_t(c - 1, t, first and s == 1)
                                if u % UNITS == 1:
                                    squares(c - 1, 1 - s, (u // UNITS,))
                        if has_next:
                            if has_prev:
                                act.wait_ge(s_t, PT * c)
                                act.wait_ge(s_sq, 3 * c)
                            start_acc(c + 1, 1 - s)
                loop(act, NCH // 2, body)
                squares(NCH - 1, 1)
                for t in range(PT):
                    evict_t(NCH - 1, t, False)

            @block.vector
            def _(dve):
                for n, (j, (dy, dx)) in enumerate(pe_taps):
                    tap = VEC_TAP + 3 * dy + dx
                    nc.vector.tensor_scalar(diag[:, n, :], ident, v128[:, j, tap:tap + 1], None, ALU.mult).then_inc(s_diag, 1)
                nc.vector.memset(gram[:, :, :], 0.0).then_inc(s_gadd, 1)

                def add_gram(c, s):
                    dve.wait_ge(s_gram, PT * (c + 1))
                    dve.wait_ge(s_gadd, c + 1)
                    nc.vector.tensor_tensor(gram[:, :, :], gram_ps[s][0:KC, 0:C].rearrange("p (a n) -> p a n", a=2), gram[:, :, :],
                                            ALU.add).then_inc(s_gadd, 1)

                def body(i, first, last):
                    for s in range(2):
                        c = 2 * i + s
                        dve.wait_ge(s_edge, 3 * (c + 1) + (3 if last and s == 1 else 0))
                        for n, (j, (dy, dx), before) in enumerate(order):
                            if before is None:
                                dve.wait_ge(s_acc, NA * c + 1 + UNITS * (2 - j))
                            else:
                                dve.wait_ge(s_dw, NDW * c + before + 1)
                            tap = VEC_TAP + 3 * dy + dx
                            a = acc[s][j][:, :].rearrange("p (r w) -> p r w", w=W)
                            nc.vector.scalar_tensor_tensor(a, yview(y[s][j], dy, dx, 0, R), v128[:, j, tap:tap + 1], a,
                                                           ALU.mult, ALU.add).then_inc(s_dw, 1)
                            if n == 5 and not first:
                                add_gram(c - 2, s)
                loop(dve, NCH // 2, body)
                add_gram(NCH - 2, 0)
                add_gram(NCH - 1, 1)
                dve.wait_ge(s_gadd, NCH + 1)


def attention_phase(nc, sb, pb, sem, *, b, NCH, gram, sq_norm, sel, mask, v96, wout, mix_a, mix_c):
    p = f"at{b}_"
    s_dve, s_root, s_norm, s_exp, s_mix = sem(p + "dve"), sem(p + "root"), sem(p + "norms"), sem(p + "exp"), sem(p + "mix")
    s_nsq, s_rn, s_neg, s_prob = sem(p + "norm_sq"), sem(p + "rnorm"), sem(p + "neg_max"), sem(p + "probs")
    with ExitStack() as ctx:
        nsq = sb(ctx, "nsq", [128, 3])
        root = sb(ctx, "root", [128, 3])
        rn = sb(ctx, "rn", [128, 3])
        ones = sb(ctx, "at_ones", [128, KC])
        rn_rows = sb(ctx, "rn_rows", [128, 3, KC])
        rq = sb(ctx, "rq", [KC, 2])
        rk = sb(ctx, "rk", [KC, 2, KC])
        logit = sb(ctx, "logit", [KC, 2, KC])
        top = sb(ctx, "top", [KC, 2])
        neg = sb(ctx, "neg", [KC, 2])
        prob = sb(ctx, "prob", [KC, 2, KC])
        total = sb(ctx, "total", [KC, 2])
        rtotal = sb(ctx, "rtotal", [KC, 2])
        ps_k = pb(ctx, "ps_k", [128, 512])
        ps_q = pb(ctx, "ps_q", [128, 512])
        ps_a = pb(ctx, "ps_a", [128, 512])
        ps_c = pb(ctx, "ps_c", [128, 512])
        half = slice(64 * b, 64 * b + 64)
        with nc.Block() as block:
            @block.tensor
            def _(pe):
                pe.wait_ge(s_rn, 1)
                for j in range(3):
                    nc.tensor.matmul(ps_k[0:KC, 0:C], rn_rows[:, j, :], sel[:, j, C:2 * C], start=(j == 0), stop=(j == 2))
                for hp in range(2):
                    for j in range(3):
                        ins = nc.tensor.matmul(ps_q[0:KC, hp:hp + 1], sel[:, j, KC * hp:KC * hp + KC], rn[:, j:j + 1],
                                               start=(j == 0), stop=(j == 2))
                ins.then_inc(s_norm, 1)
                pe.wait_ge(s_prob, 2)
                nc.tensor.matmul(ps_a[0:96, 0:C], prob[:, 0, :], wout[:, 0, :], start=True, stop=True)
                nc.tensor.matmul(ps_a[96:128, 0:C], prob[:, 1, 0:32], wout[:, 1, :], start=True, stop=True)
                nc.tensor.matmul(ps_c[half, 0:C], prob[:, 1, 32:96], wout[:, 1, :], start=True, stop=True).then_inc(s_mix, 1)

            @block.scalar
            def _(act):
                act.wait_ge(s_nsq, 1)
                nc.scalar.activation(root[:, :], nsq[:, :], ACT.Sqrt).then_inc(s_root, 1)
                act.wait_ge(s_neg, 1)
                for hp in range(2):
                    nc.scalar.activation(prob[:, hp, :], logit[:, hp, :], ACT.Exp, bias=neg[:, hp:hp + 1],
                                         accum_out=total[:, hp:hp + 1]).then_inc(s_exp, 1)

            @block.vector
            def _(dve):
                n = [0]

                def link(ins):
                    n[0] += 1
                    ins.then_inc(s_dve, 1)
                    dve.wait_ge(s_dve, n[0])
                link(nc.vector.memset(ones[:, :], 1.0))
                link(nc.vector.memset(mix_c[:, :], 0.0))
                nc.vector.reduce_sum(nsq[:, :], sq_norm[:, :, :], AX.X).then_inc(s_nsq, 1)
                dve.wait_ge(s_root, 1)
                link(nc.vector.tensor_scalar_max(root[:, :], root[:, :], 1e-12))
                link(nc.vector.reciprocal(rn[:, :], root[:, :]))
                for j in range(3):
                    ins = nc.vector.tensor_scalar(rn_rows[:, j, :], ones[:, :], rn[:, j:j + 1], None, ALU.mult)
                ins.then_inc(s_rn, 1)
                dve.wait_ge(s_norm, 1)
                link(nc.vector.tensor_copy(rk[:, :, :], ps_k[0:KC, 0:C].rearrange("p (a n) -> p a n", a=2)))
                link(nc.vector.tensor_tensor(rq[:, :], ps_q[0:KC, 0:2], v96[:, :, V_TEMP], ALU.mult))
                for hp in range(2):
                    link(nc.vector.scalar_tensor_tensor(logit[:, hp, :], gram[:, hp, :], rq[:, hp:hp + 1], rk[:, hp, :],
                                                        ALU.mult, ALU.mult))
                    link(nc.vector.tensor_tensor(logit[:, hp, :], logit[:, hp, :], mask[:, :], ALU.add))
                    link(nc.vector.reduce_max(top[:, hp:hp + 1], logit[:, hp, :], AX.X))
                nc.vector.tensor_scalar(neg[:, :], top[:, :], -1.0, None, ALU.mult).then_inc(s_neg, 1)
                dve.wait_ge(s_exp, 2)
                link(nc.vector.reciprocal(rtotal[:, :], total[:, :]))
                for hp in range(2):
                    nc.vector.tensor_scalar(prob[:, hp, :], prob[:, hp, :], rtotal[:, hp:hp + 1], None, ALU.mult).then_inc(s_prob, 1)
                dve.wait_ge(s_mix, 1)
                for dst, src in ((slice(0, C), slice(0, C)),) if b == 0 else ((slice(0, C - 128), slice(128, C)),
                                                                              (slice(C - 128, C), slice(0, 128))):
                    link(nc.vector.tensor_copy(mix_a[:, dst], ps_a[:, src]))
                    link(nc.vector.tensor_copy(mix_c[half, dst], ps_c[half, src]))


def v_phase(nc, sb, pb, sem, loop, *, NPX, UNITS, UR, NCH, PT, H, W, x_cm, x_px, x1_d, x_in, y, acc, wfold, bias_y,
            bias_yc, v128, mix_a, mix_c, x1_sq, x1_mean, moments, sel):
    NU = 3 * UNITS
    NY = NU + UNITS
    assert NY % 2 == 0
    ops = dve_order(V_PE_TAPS)
    NDW = len(ops)
    HPX = NPX // 2
    HU = UNITS // 2
    QT = PT // 2
    MU = B * PT // 2
    QM = QT // 2
    s_row0, s_one, s_edge = sem("v_row0"), sem("v_ones"), sem("v_edge_rows")
    s_load = [sem(f"v_load{s}") for s in range(2)]
    s_res = [sem(f"v_residual{s}") for s in range(4)]
    s_store = [sem(f"v_store{s}") for s in range(4)]
    s_y, s_yev = sem("v_y_ready"), sem("v_y_evicted")
    s_acc, s_dw, s_diag = sem("v_acc_started"), sem("v_dw_ops"), sem("v_diag")
    s_mix, s_x1, s_sq, s_st, s_sadd = sem("v_mixed"), sem("v_x1"), sem("v_squared"), sem("v_stat_units"), sem("v_sums_added")
    with ExitStack() as ctx:
        x_row0 = sb(ctx, "v_x_row0", [KC, 2, B, W])
        res = [sb(ctx, f"res{s}", [128, QT, C]) for s in range(4)]
        sq = [sb(ctx, f"sq{s}", [128, 2, C]) for s in range(4)]
        ones = sb(ctx, "v_ones", [128, 1])
        v_sums = sb(ctx, "v_sums", [128, 3, NCH])
        v_total = sb(ctx, "v_total", [128, 3])
        diag = sb(ctx, "v_diag", [128, len(V_PE_TAPS[0]), 128])
        y_ps = [pb(ctx, f"vy_ps{s}", [128, 512]) for s in range(2)]
        mix_ps = [pb(ctx, f"mix_ps{s}", [128, 512]) for s in range(4)]
        st_ps = [pb(ctx, f"st_ps{s}", [128, 512]) for s in range(2)]
        x_half = [x_in[s][:, :, :].rearrange("c k (b n) -> c k b n", b=B) for s in range(2)]
        mix_after = [range(min(u * MU // (NU - 2), MU), min((u + 1) * MU // (NU - 2), MU)) for u in range(NU)]
        order = [(h, q, j) for h in range(2) for q in range(HU) for j in range(3)]

        def image_of(m):
            quarter, r = m // QM, m % QM
            h, b = quarter // 2, quarter % 2
            return quarter, b, h * HPX + r * 256, r

        with nc.Block() as block:
            @block.sync
            def _(sp):
                src = [x_cm[b].rearrange("(k c) n -> c k n", k=2) for b in range(B)]
                px = [x_px.rearrange("(t p) c -> p t c", p=128)[:, :, C * b:C * b + C] for b in range(B)]
                dst = [x1_d.rearrange("(t p) c -> p t c", p=128)[:, :, C * b:C * b + C] for b in range(B)]
                for b in range(B):
                    sp.dma_start(x_row0[:, :, b, :], src[b][:, :, 0:W]).then_inc(s_row0, 16)

                def load_half(c, h):
                    for b in range(B):
                        sp.dma_start(x_half[h][:, :, b, :], src[b][:, :, bass.ds(c * NPX + W + h * HPX, HPX)]).then_inc(s_load[h], 16)

                def load_residual(c, quarter):
                    h, b = quarter // 2, quarter % 2
                    sp.dma_start(res[quarter][:, :, :], px[b][:, bass.ds(c * PT + h * QT, QT), :]).then_inc(s_res[quarter], 16)

                def store(c, quarter):
                    h, b = quarter // 2, quarter % 2
                    sp.wait_ge(s_x1, MU * c + QM * (quarter + 1))
                    sp.dma_start(dst[b][:, bass.ds(c * PT + h * QT, QT), :], res[quarter][:, :, :]).then_inc(s_store[quarter], 16)

                def reload(c, quarter):
                    sp.wait_ge(s_store[quarter], 16 * c)
                    sp.wait_ge(s_st, MU * (c - 1) + QM * (quarter + 1))
                    load_residual(c, quarter)

                for h in range(2):
                    load_half(0, h)
                for quarter in range(4):
                    load_residual(0, quarter)
                for h in range(2):
                    sp.wait_ge(s_y, 4 + NU // 2 * (h + 1))
                    load_half(1, h)

                def body(i, first, last):
                    for s in range(2):
                        c = 2 * i + s
                        has_prev = not (first and s == 0)
                        for h in range(2):
                            if has_prev:
                                store(c - 1, 2 * h)
                                if h == 1:
                                    reload(c, 1)
                                store(c - 1, 2 * h + 1)
                                reload(c, 2 * h)
                            if not last:
                                sp.wait_ge(s_y, 4 + NY * (c + 1) + NU // 2 * (h + 1))
                                load_half(c + 2, h)
                        if has_prev:
                            reload(c, 3)
                loop(sp, NCH // 2, body)
                for quarter in range(4):
                    store(NCH - 1, quarter)
                for quarter in range(4):
                    sp.wait_ge(s_store[quarter], 16 * NCH)

            @block.gpsimd
            def _(pool):
                nc.gpsimd.memset(ones[:, :], 1.0).then_inc(s_one, 1)
                for j in range(3):
                    nc.gpsimd.memset(y[0][j][:, 0, :], 0.0).then_inc(s_edge, 1)

                pool.wait_ge(s_yev, 4 + NY * (NCH - 1) + NU)
                for j in range(3):
                    nc.gpsimd.memset(y[1][j][:, R + 1, :], 0.0).then_inc(s_edge, 1)

            @block.tensor
            def _(pe):
                def project(j, dst, xt, px0, n):
                    if j < 2:
                        for k in range(2):
                            ins = nc.tensor.matmul(dst[:, 0:n], wfold[j][:, k, 384:512], xt[:, k, j, px0:px0 + n],
                                                   start=(k == 0), stop=(k == 1))
                    else:
                        for k in range(2):
                            for b in range(B):
                                ins = nc.tensor.matmul(dst[64 * b:64 * b + 64, 0:n], wfold[b][:, k, 512:576],
                                                       xt[:, k, b, px0:px0 + n], start=(k == 0), stop=(k == 1))
                    ins.then_inc(s_y, 1)

                def conv_unit(c, n):
                    pe.wait_ge(s_yev, NY * c + n + 4 - 1)
                    h, q, j = order[n]
                    project(j, y_ps[n % 2], x_half[h], q * 512, 512)

                def taps(c, s):
                    pe.wait_ge(s_edge, 3 * (c + 1))
                    for q in range(UNITS):
                        pe.wait_ge(s_yev, 4 + NY * c + max(NU, NU + q - 1))
                        for n, (dy, dx) in enumerate(V_PE_TAPS[0]):
                            ins = nc.tensor.matmul(y_ps[(NU + q) % 2][:, :], diag[:, n, :], y[s][0][:, dy + q * UR:dy + q * UR + UR, dx:dx + W],
                                                   start=(n == 0), stop=(n == len(V_PE_TAPS[0]) - 1))
                        ins.then_inc(s_y, 1)

                def mix_unit(c, s, m, early):
                    quarter, b, px0, r = image_of(m)
                    if not (early and m < 4):
                        pe.wait_ge(s_x1, MU * c + m - 3)
                    for t in range(2):
                        px = slice(px0 + 128 * t, px0 + 128 * t + 128)
                        nc.tensor.matmul(mix_ps[m % 4][:, C * t:C * t + C], acc[s][b][:, px], mix_a[b][:, :], start=True, stop=False,
                                         skip_group_check=True)
                        ins = nc.tensor.matmul(mix_ps[m % 4][:, C * t:C * t + C], acc[s][2][:, px], mix_c[b][:, :], start=False,
                                               stop=True, skip_group_check=True)
                    ins.then_inc(s_mix, 1)

                def stat_unit(c, s, m):
                    quarter, b, px0, r = image_of(m)
                    pe.wait_ge(s_sq, MU * c + m + 1)
                    for t in range(2):
                        for k in range(2):
                            col = 2 * k + b
                            ins = nc.tensor.matmul(st_ps[s][0:KC, col:col + 1], sq[m % 4][:, t, KC * k:KC * k + KC], ones[:, :],
                                                   start=(m == 0 and t == 0 and k == 0),
                                                   stop=(m == MU - 1 and t == 1 and k == 1), skip_group_check=True)
                    ins.then_inc(s_st, 1)

                def mix_begin(c, early):
                    pe.wait_ge(s_dw, NDW * (c + 1))
                    if not early:
                        pe.wait_ge(s_sadd, c)

                def mix_step(c, s, m, early):
                    mix_unit(c, s, m, early)
                    if m >= 4:
                        stat_unit(c, s, m - 4)

                pe.wait_ge(s_row0, 32)
                for n in range(4):
                    if n >= 2:
                        pe.wait_ge(s_yev, n - 1)
                    project(n % 3, y_ps[n % 2], x_row0, 0, W)
                pe.wait_ge(s_one, 1)
                for n in range(NU):
                    if n == 0 or n == NU // 2:
                        pe.wait_ge(s_load[n // (NU // 2)], 32)
                    conv_unit(0, n)
                pe.wait_ge(s_diag, len(V_PE_TAPS[0]))
                taps(0, 0)

                def body(i, first, last):
                    for s in range(2):
                        c = 2 * i + s
                        has_next = not (last and s == 1)
                        has_prev = not (first and s == 0)
                        if has_prev:
                            mix_begin(c - 1, first)
                        for n in range(NU):
                            if has_next:
                                if n == 0 or n == NU // 2:
                                    pe.wait_ge(s_load[n // (NU // 2)], 32 * (c + 2))
                                conv_unit(c + 1, n)
                            if has_prev:
                                for m in mix_after[n]:
                                    mix_step(c - 1, 1 - s, m, first and s == 1)
                        if has_prev:
                            for m in range(MU - 4, MU):
                                stat_unit(c - 1, 1 - s, m)
                        if has_next:
                            taps(c + 1, 1 - s)
                loop(pe, NCH // 2, body)
                mix_begin(NCH - 1, False)
                for m in range(MU):
                    mix_step(NCH - 1, 1, m, False)
                for m in range(MU - 4, MU):
                    stat_unit(NCH - 1, 1, m)

            @block.scalar
            def _(act):
                def bias(j):
                    return bias_y[:, 3, j:j + 1] if j < 2 else bias_yc[:, :]

                def taps(j):
                    return 3 if j < 2 else 4

                def evict_y(c, s, n):
                    h, q, j = order[n]
                    r0 = 2 + (h * HU + q) * UR
                    act.wait_ge(s_y, 4 + NY * c + n + 1)
                    nc.scalar.activation(y[s][j][:, r0:r0 + UR, 1:W + 1], y_ps[n % 2][:, :].rearrange("p (r w) -> p r w", w=W),
                                         ACT.Identity, bias=bias(j)).then_inc(s_yev, 1)

                def square(c, m, early):
                    quarter, b, px0, r = image_of(m)
                    act.wait_ge(s_x1, MU * c + m + 1)
                    if m >= 4 or not early:
                        act.wait_ge(s_st, MU * c + m - 3)
                    nc.scalar.activation(sq[m % 4][:, :, :], res[quarter][:, 2 * r:2 * r + 2, :], ACT.Square).then_inc(s_sq, 1)

                def start_acc(c, s):
                    act.wait_ge(s_edge, 3 * (c + 1))
                    act.wait_ge(s_yev, 4 + NY * c + NU)
                    for j in (1, 2):
                        nc.scalar.activation(acc[s][j][:, :].rearrange("p (r w) -> p r w", w=W), y[s][j][:, 0:R, 0:W],
                                             ACT.Identity, scale=v128[:, taps(j), VEC_TAP:VEC_TAP + 1],
                                             bias=v128[:, taps(j), VEC_BDW:VEC_BDW + 1]).then_inc(s_acc, 1)
                    for q in range(UNITS):
                        act.wait_ge(s_y, 4 + NY * c + NU + q + 1)
                        nc.scalar.activation(acc[s][0][:, q * 512:(q + 1) * 512], y_ps[(NU + q) % 2][:, :], ACT.Identity,
                                             bias=v128[:, taps(0), VEC_BDW:VEC_BDW + 1]).then_inc(s_yev, 1)

                for n in range(4):
                    act.wait_ge(s_y, n + 1)
                    nc.scalar.activation(y[0][n % 3][:, 1, 1:W + 1], y_ps[n % 2][:, 0:W], ACT.Identity, bias=bias(n % 3)).then_inc(s_yev, 1)
                for n in range(NU):
                    evict_y(0, 0, n)
                start_acc(0, 0)

                def body(i, first, last):
                    for s in range(2):
                        c = 2 * i + s
                        has_next = not (last and s == 1)
                        has_prev = not (first and s == 0)
                        if has_next:
                            if has_prev:
                                act.wait_ge(s_dw, NDW * c)
                            act.wait_ge(s_yev, 4 + NY * c + NU)
                            for j in range(3):
                                nc.scalar.activation(y[1 - s][j][:, 0:2, 1:W + 1], y[s][j][:, R:R + 2, 1:W + 1], ACT.Copy).then_inc(s_edge, 1)
                        for n in range(NU):
                            if has_next:
                                evict_y(c + 1, 1 - s, n)
                            if has_prev:
                                for m in mix_after[n]:
                                    square(c - 1, m, first and s == 1)
                        if has_next:
                            if has_prev:
                                act.wait_ge(s_mix, MU * c)
                            start_acc(c + 1, 1 - s)
                loop(act, NCH // 2, body)
                for m in range(MU):
                    square(NCH - 1, m, False)

            @block.vector
            def _(dve):
                nc.vector.memset(x1_sq[:, :], 0.0).then_inc(s_sadd, 1)

                for n, (dy, dx) in enumerate(V_PE_TAPS[0]):
                    tap = VEC_TAP + 3 * dy + dx
                    nc.vector.tensor_scalar(diag[:, n, :], sel[:, 0, 0:128], v128[:, 3, tap:tap + 1], None, ALU.mult).then_inc(s_diag, 1)

                def add_residual(c, m):
                    quarter, b, px0, r = image_of(m)
                    dve.wait_ge(s_mix, MU * c + m + 1)
                    if r == 0:
                        dve.wait_ge(s_res[quarter], 16 * (c + 1))
                    x = res[quarter][:, 2 * r:2 * r + 2, :]
                    nc.vector.tensor_tensor(x, mix_ps[m % 4][:, 0:2 * C].rearrange("p (t c) -> p t c", t=2), x, ALU.add).then_inc(s_x1, 1)

                def add_sums(c, s):
                    dve.wait_ge(s_st, MU * (c + 1))
                    dve.wait_ge(s_sadd, c + 1)
                    nc.vector.tensor_tensor(x1_sq[:, :], st_ps[s][0:KC, 0:4], x1_sq[:, :], ALU.add).then_inc(s_sadd, 1)

                mix_at = [[m for m in range(MU) if 2 + m * (NDW - 7) // MU == n] for n in range(NDW)]

                def body(i, first, last):
                    for s in range(2):
                        c = 2 * i + s
                        has_prev = not (first and s == 0)
                        dve.wait_ge(s_edge, 3 * (c + 1) + (3 if last and s == 1 else 0))
                        for n, (j, (dy, dx), before) in enumerate(ops):
                            if before is not None:
                                dve.wait_ge(s_dw, NDW * c + before + 1)
                            elif j == 0:
                                dve.wait_ge(s_yev, 4 + NY * (c + 1))
                            else:
                                dve.wait_ge(s_acc, 2 * c + j)
                            tap = VEC_TAP + 3 * dy + dx
                            a = acc[s][j][:, :].rearrange("p (r w) -> p r w", w=W)
                            total = v_sums[:, j, bass.ds(c, 1)] if (dy, dx) == ALL_TAPS[-1] else None
                            nc.vector.scalar_tensor_tensor(a, y[s][j][:, dy:dy + R, dx:dx + W], v128[:, 3 if j < 2 else 4, tap:tap + 1],
                                                           a, ALU.mult, ALU.add, accum_out=total).then_inc(s_dw, 1)
                            if has_prev:
                                for m in mix_at[n]:
                                    add_residual(c - 1, m)
                            if n == 3 and not first:
                                add_sums(c - 2, s)
                loop(dve, NCH // 2, body)
                add_sums(NCH - 2, 0)
                for m in range(MU):
                    add_residual(NCH - 1, m)
                add_sums(NCH - 1, 1)
                dve.wait_ge(s_sadd, NCH + 1)

        s_total, s_vmean, s_raw = sem("v_total"), sem("v_mixed_mean"), sem("v_mean_raw")
        s_order, s_mean = sem("v_reordered"), sem("v_mean")
        with nc.Block() as block:
            @block.tensor
            def _(pe):
                pe.wait_ge(s_total, 1)
                for k in range(2):
                    for b in range(B):
                        half = slice(KC * k, KC * k + KC)
                        col = slice(2 * k + b, 2 * k + b + 1)
                        nc.tensor.matmul(st_ps[0][0:KC, col], mix_a[b][:, half], v_total[:, b:b + 1], start=True, stop=False,
                                         skip_group_check=True)
                        ins = nc.tensor.matmul(st_ps[0][0:KC, col], mix_c[b][:, half], v_total[:, 2:3], start=False, stop=True,
                                               skip_group_check=True)
                ins.then_inc(s_vmean, 1)
                pe.wait_ge(s_raw, 1)
                for n, sums in enumerate((x1_sq, x1_mean)):
                    for k in range(2):
                        for src, shift in ((k, 192), (1 - k, 96)):
                            ins = nc.tensor.matmul(st_ps[1][0:KC, 2 * n + k:2 * n + k + 1], sel[0:KC, 1, shift:shift + KC],
                                                   sums[:, 2 * src + 1:2 * src + 2], start=(src == k), stop=(src != k),
                                                   skip_group_check=True)
                ins.then_inc(s_order, 1)

            @block.vector
            def _(dve):
                nc.vector.tensor_reduce(v_total[:, :], v_sums[:, :, :], AX.X, ALU.add).then_inc(s_total, 1)
                dve.wait_ge(s_vmean, 1)
                nc.vector.tensor_copy(x1_mean[:, :], st_ps[0][0:KC, 0:4]).then_inc(s_raw, 1)
                dve.wait_ge(s_order, 1)
                nc.vector.tensor_copy(x1_sq[:, 1:4:2], st_ps[1][0:KC, 0:2]).then_inc(s_mean, 1)
                nc.vector.tensor_copy(x1_mean[:, 1:4:2], st_ps[1][0:KC, 2:4]).then_inc(s_mean, 1)
                dve.wait_ge(s_mean, 2)
                nc.vector.scalar_tensor_tensor(x1_mean[:, :], x1_mean[:, :], 1.0 / (H * W), moments[:, :, 0],
                                               ALU.mult, ALU.add).then_inc(s_mean, 1)
                dve.wait_ge(s_mean, 3)


def scan_coefficients(nc, sb, pb, sem, *, H, W, x1_sq, x1_mean, v96, v_scan, sel, gavg, scale, shift, gn_tmp,
                      moments, co):
    s_mom, s_dve = sem("p2_mom"), sem("p2_dve")
    gn_sems = [sem(f"p2_gn{i}") for i in range(4)]
    inv = 1.0 / (H * W)
    with ExitStack() as ctx:
        ps = pb(ctx, "p2_ps", [128, 16])
        with nc.Block() as block:
            @block.vector
            def _(dve):
                n = [0]

                def link(ins):
                    n[0] += 1
                    ins.then_inc(s_dve, 1)
                    dve.wait_ge(s_dve, n[0])
                for k in range(2):
                    for b in range(B):
                        a = 2 * k + b
                        bo = v96[:, k, V_BOUT:V_BOUT + 1]
                        m, q = moments[:, a, 0:1], moments[:, a, 1:2]
                        t = gn_tmp[:, a:a + 1]
                        link(nc.vector.tensor_copy(m, x1_mean[:, a:a + 1]))
                        link(nc.vector.tensor_scalar(q, x1_sq[:, a:a + 1], inv, None, ALU.mult))
                        link(nc.vector.scalar_tensor_tensor(t, m, 2.0, bo, ALU.mult, ALU.add))
                        link(nc.vector.scalar_tensor_tensor(q, t, bo, q, ALU.mult, ALU.add))
                        link(nc.vector.tensor_tensor(m, m, bo, ALU.add))
                nc.vector.tensor_copy(gn_tmp[:, 0:1], moments[:, 0, 0:1]).then_inc(s_mom, 1)

        with nc.Block() as block:
            group_norm_scale(nc, block, moments, (s_mom, 1), ps, gn_tmp, scale, shift, gavg, 1e-5, gn_sems)

        s_tiles, s_moved = sem("p2_tiles"), sem("p2_moved")
        with nc.Block() as block:
            @block.tensor
            def _(pe):
                for q, t in enumerate((scale, shift)):
                    for b in range(B):
                        nc.tensor.matmul(ps[:, 2 * b + q:2 * b + q + 1], sel[0:KC, 0, 0:128], t[:, b:b + 1], start=True, stop=False,
                                         skip_group_check=True)
                        nc.tensor.matmul(ps[:, 2 * b + q:2 * b + q + 1], sel[0:KC, 1, 128 - KC:256 - KC], t[:, B + b:B + b + 1],
                                         start=False, stop=True, skip_group_check=True)
                        ins = nc.tensor.matmul(ps[64 * b:64 * b + 64, 4 + q:5 + q], sel[0:KC, 1, 256 - KC:320 - KC],
                                               t[:, B + b:B + b + 1], start=True, stop=True, skip_group_check=True)
                ins.then_inc(s_tiles, 1)

            @block.vector
            def _(dve):
                dve.wait_ge(s_tiles, 1)
                nc.vector.tensor_copy(co["scale_shift"][:, :, :], ps[:, 0:6].rearrange("p (j q) -> p j q", q=2)).then_inc(s_moved, 1)
                dve.wait_ge(s_moved, 1)

        s_co = sem("p2_co")
        with nc.Block() as block:
            @block.vector
            def _(dve):
                n = [0]

                def link(ins):
                    n[0] += 1
                    ins.then_inc(s_co, 1)
                    dve.wait_ge(s_co, n[0])
                for j in range(3):
                    def col(t):
                        return t[:, j:j + 1]
                    scale_j, shift_j = co["scale_shift"][:, j, 0:1], co["scale_shift"][:, j, 1:2]
                    bo, bv = v_scan[:, j, V_BOUT:V_BOUT + 1], v_scan[:, j, V_BV:V_BV + 1]
                    link(nc.vector.scalar_tensor_tensor(col(co["c_base"]), scale_j, bo, shift_j, ALU.mult, ALU.add))
                    link(nc.vector.tensor_scalar(col(co["c_tmp"]), v_scan[:, j, V_DV:V_DV + 1], v_scan[:, j, V_RES:V_RES + 1], None, ALU.add))
                    link(nc.vector.tensor_tensor(col(co["u_mul"]), scale_j, bv, ALU.mult))
                    link(nc.vector.tensor_tensor(col(co["u_add"]), col(co["c_base"]), bv, ALU.mult))
                    link(nc.vector.tensor_tensor(col(co["d_mul"]), scale_j, col(co["c_tmp"]), ALU.mult))
                    link(nc.vector.tensor_tensor(col(co["d_add"]), col(co["c_base"]), col(co["c_tmp"]), ALU.mult))
                    link(nc.vector.tensor_scalar(col(co["e_mul"]), col(co["d_mul"]), 2.0, 1.0, ALU.mult, ALU.add))
                    link(nc.vector.scalar_tensor_tensor(col(co["e_add"]), col(co["d_add"]), 2.0, bo, ALU.mult, ALU.add))


T = 8


def scan_phase(nc, sb, pb, sem, loop, *, along_w, H, W, HT, x1_d, part_d, out, amat, v_scan, co, ident):
    N = W if along_w else W + 2
    LO = C - 128
    p = "w_" if along_w else "h_"
    G = 4
    PAIRS = T // 2
    s_zero = sem(p + "zero")
    s_load = [sem(f"{p}load{s}") for s in range(2)]
    s_part = [sem(f"{p}part{s}") for s in range(2)]
    s_store = [sem(f"{p}store{s}") for s in range(2)]
    s_xt, s_u = sem(p + "x_transposed"), sem(p + "u_ready")
    s_mm_wide, s_mm_shared = sem(p + "products_wide"), sem(p + "products_shared")
    s_h_wide, s_h_shared = sem(p + "state_wide"), sem(p + "state_shared")
    s_z, s_zt, s_out = sem(p + "z"), sem(p + "z_transposed"), sem(p + "out")
    s_dcol, s_dz = sem(p + "diag_in"), sem(p + "diag_out")
    s_dload, s_dxt, s_dev = sem(p + "diag_load"), sem(p + "diag_transposed"), sem(p + "diag_evicted")

    def channels(t, j):
        return t[:, j, 0:128] if j < 2 else t[:, :, 128:C]

    x1_tile = [slice(0, 128), slice(2 * 128, 3 * 128), slice(128, 2 * 128)]

    def step_tile(t, tt, h):
        return t[:, h, :, tt, :] if along_w else t[:, :, tt, h, :]

    with ExitStack() as ctx:
        gshape = [128, HT, B, G, C] if along_w else [128, B, G, HT, C]
        xs = [sb(ctx, f"{p}x{s}", [128, HT, G, B * C] if along_w else [128, G, HT, B * C]) for s in range(2)]
        os = [sb(ctx, f"{p}o{s}", gshape) for s in range(2)]
        u = sb(ctx, f"{p}u", [128, 3, T, N])
        z = sb(ctx, f"{p}z", [128, 3, T, W])
        hs = sb(ctx, f"{p}h", [128, 3, T, N])
        if not along_w:
            u_diag = sb(ctx, "u_diag", [128, 3, H, 2])
            e_diag = sb(ctx, "e_diag", [128, 3, H, 2])
            z_diag = sb(ctx, "z_diag", [128, 3, H, 2])
            px_diag = sb(ctx, "px_diag", [128, 2, HT, B * C])
        wide_ps = pb(ctx, p + "wide_ps", [128, 2, 512])
        shared_ps = pb(ctx, p + "shared_ps", [128, 512])
        x_ps = [pb(ctx, f"{p}x_ps{j}", [128, 512]) for j in range(3)]
        o_ps = [pb(ctx, f"{p}o_ps{h}", [128, 512]) for h in range(HT)]

        def pixels_first(h):
            return o_ps[h][:, 0:B * C].rearrange("p (b c) -> p b c", b=B)

        def by_group(d):
            if along_w:
                return d.rearrange("(h p w) c -> p h w c", p=128, w=W)
            return d.rearrange("(y h p) c -> p y h c", p=128, h=HT)

        def group(view, n):
            return view[:, :, bass.ds(n * G, G), :] if along_w else view[:, bass.ds(n * G, G), :, :]

        def image(t, b):
            return t[:, :, b, :, :] if along_w else t[:, b, :, :, :]

        def diagonal(d, which, h):
            step = W + 1 if which == 0 else W - 1
            start = (0 if which == 0 else W - 1) + 128 * h * step
            return d[start:start + 127 * step + 1:step, :]

        if not along_w:
            with nc.Block() as block:
                @block.sync
                def _(sp):
                    for d in range(2):
                        for h in range(HT):
                            sp.dma_start(px_diag[:, d, h, :], diagonal(x1_d, d, h)).then_inc(s_dload, 16)

                @block.tensor
                def _(pe):
                    pe.wait_ge(s_dload, 16 * 2 * HT)
                    for d in range(2):
                        for j in range(3):
                            if d > 0:
                                pe.wait_ge(s_dev, 2 * (j + 1))
                            for h in range(HT):
                                ins = nc.tensor.transpose(x_ps[j][:, h * 128:h * 128 + 128], px_diag[:, d, h, x1_tile[j]], ident)
                            ins.then_inc(s_dxt, 1)

                @block.scalar
                def _(act):
                    for d in range(2):
                        for j in range(3):
                            act.wait_ge(s_dxt, 3 * d + j + 1)
                            src = x_ps[j][:, 0:H]
                            nc.scalar.activation(u_diag[:, j, :, d], src, ACT.Identity, scale=co["u_mul"][:, j:j + 1],
                                                 bias=co["u_add"][:, j:j + 1]).then_inc(s_dev, 1)
                            nc.scalar.activation(e_diag[:, j, :, d], src, ACT.Identity, scale=co["d_mul"][:, j:j + 1],
                                                 bias=co["d_add"][:, j:j + 1]).then_inc(s_dev, 1)

        with nc.Block() as block:
            @block.sync
            def _(sp):
                xv = by_group(x1_d)
                pv = [by_group(part_d[b]) for b in range(B)]

                def load_x(n, s, wait):
                    if wait:
                        sp.wait_ge(s_xt, 3 * G // 2 * (n - 1))
                    sp.dma_start(xs[s][:, :, :, :], group(xv, n)).then_inc(s_load[s], 16)

                def load_part(n, i, s, wait):
                    if wait:
                        sp.wait_ge(s_store[s], 32 * i)
                    for b in range(B):
                        sp.dma_start(image(os[s], b), group(pv[b], n)).then_inc(s_part[s], 16)

                load_x(0, 0, False)

                def body(i, first, last):
                    for s in range(2):
                        if not (last and s == 1):
                            load_x(2 * i + s + 1, 1 - s, not (first and s == 0))
                        if along_w:
                            load_part(2 * i + s, i, s, not first)
                loop(sp, H // T, body)

            @block.gpsimd
            def _(pool):
                ov = [by_group((out if along_w else part_d)[b]) for b in range(B)]
                nc.gpsimd.memset(hs[:, :, T - 1, :], 0.0).then_inc(s_zero, 1)

                def store(n, s):
                    pool.wait_ge(s_out, HT * G * (n + 1))
                    for b in range(B):
                        pool.dma_start(group(ov[b], n), image(os[s], b)).then_inc(s_store[s], 16)

                def body(i, first, last):
                    store(2 * i, 0)
                    store(2 * i + 1, 1)
                loop(pool, H // T, body)
                for s in range(2):
                    pool.wait_ge(s_store[s], 32 * (H // T))

            @block.tensor
            def _(pe):
                def transpose_x(i, P, j, wait_bank):
                    if j == 0 and P % 2 == 0:
                        pe.wait_ge(s_load[(P // 2) % 2], 16 * (i + P // PAIRS + 1))
                    if wait_bank:
                        pe.wait_ge(s_u, 3 * (PAIRS * i + P - 1) + j + 1)
                    for tt in range(2):
                        for h in range(HT):
                            col = (tt * HT + h) * 128
                            x = xs[(P // 2) % 2]
                            step = 2 * (P % 2) + tt
                            ins = nc.tensor.transpose(x_ps[j][:, col:col + 128],
                                                      x[:, h, step, x1_tile[j]] if along_w else x[:, step, h, x1_tile[j]], ident)
                    ins.then_inc(s_xt, 1)

                def transpose_z(i, t):
                    if t % 2 == 0:
                        pe.wait_ge(s_z, 3 * (PAIRS * i + t // 2) + 3)
                    for h in range(HT):
                        if not (isinstance(i, int) and T * i + t <= 0):
                            pe.wait_ge(s_out, HT * (T * i + t - 1) + h + 1)
                        for j in range(3):
                            ins = nc.tensor.transpose(channels(pixels_first(h), j), z[:, j, t % T, 128 * h:128 * h + 128], ident)
                        ins.then_inc(s_zt, 1)

                for j in range(3):
                    transpose_x(0, 0, j, False)
                pe.wait_ge(s_zero, 1)

                def body(i, first, last):
                    for t in range(T):
                        prev = (t - 1) % T
                        if not (first and t == 0):
                            pe.wait_ge(s_h_wide, T * i + t)
                        for b in range(B):
                            nc.tensor.matmul(wide_ps[:, b, 0:N], amat[:, 0, :], hs[:, b, prev, :], start=True, stop=False,
                                             skip_group_check=True)
                        if not (first and t == 0):
                            pe.wait_ge(s_h_shared, T * i + t)
                        for b in range(B):
                            rows = slice(LO * b, LO * b + LO)
                            ins = nc.tensor.matmul(wide_ps[:, b, 0:N], amat[rows, 1, :], hs[rows, 2, prev, :], start=False, stop=True,
                                                   skip_group_check=True)
                        ins.then_inc(s_mm_wide, 1)
                        nc.tensor.matmul(shared_ps[:, 0:N], amat[:, 2, :], hs[:, 2, prev, :], start=True, stop=False,
                                         skip_group_check=True)
                        for b in range(B):
                            rows = slice(LO * b, LO * b + LO)
                            ins = nc.tensor.matmul(shared_ps[rows, 0:N], amat[:, 3, 0:LO], hs[:, b, prev, :], start=False, stop=True,
                                                   skip_group_check=True)
                        ins.then_inc(s_mm_shared, 1)
                        if not (last and t >= T - 2):
                            for j in ((0, 1) if t % 2 == 0 else (2,)):
                                transpose_x(i, t // 2 + 1, j, True)
                        if not (first and t < 3):
                            transpose_z(i, t - 3)
                loop(pe, H // T, body)
                for t in range(T - 3, T):
                    transpose_z(H // T - 1, t)

            @block.scalar
            def _(act):
                def make_u(i, P, j):
                    q = P % PAIRS
                    act.wait_ge(s_xt, 3 * (PAIRS * i + P) + j + 1)
                    if not (isinstance(i, int) and PAIRS * i + P < PAIRS):
                        before = PAIRS * i + P - PAIRS
                        act.wait_ge(s_h_wide if j < 2 else s_h_shared, 2 * before + 2)
                        if along_w:
                            act.wait_ge(s_zt, HT * (2 * before + 2))
                    src = x_ps[j][:, 0:2 * W].rearrange("p (t n) -> p t n", t=2)
                    ins = nc.scalar.activation(u[:, j, 2 * q:2 * q + 2, 0:W], src, ACT.Identity, scale=co["u_mul"][:, j:j + 1],
                                               bias=co["u_add"][:, j:j + 1])
                    if along_w:
                        ins = nc.scalar.activation(z[:, j, 2 * q:2 * q + 2, :], src, ACT.Identity, scale=co["e_mul"][:, j:j + 1],
                                                   bias=co["e_add"][:, j:j + 1])
                    ins.then_inc(s_u, 1)

                def evict_out(i, t):
                    slot = (t // G) % 2
                    for h in range(HT):
                        act.wait_ge(s_zt, HT * (T * i + t) + h + 1)
                        if h == 0 and t % G == 0 and not (isinstance(i, int) and T * i + t < T):
                            act.wait_ge(s_store[slot], 32 * i)
                        nc.scalar.activation(step_tile(os[slot], t % G, h), pixels_first(h), ACT.Copy).then_inc(s_out, 1)

                for j in range(3):
                    make_u(0, 0, j)

                def body(i, first, last):
                    for t in range(T):
                        if not (last and t >= T - 2):
                            for j in ((0, 1) if t % 2 == 0 else (2,)):
                                make_u(i, t // 2 + 1, j)
                        if not along_w and not (first and t < 3):
                            evict_out(i, t - 3)
                loop(act, H // T, body)
                if not along_w:
                    for t in range(T - 3, T):
                        evict_out(H // T - 1, t)

            @block.vector
            def _(dve):
                def wide_state(i, t, first):
                    pair = PAIRS * i + t // 2
                    dve.wait_ge(s_mm_wide, T * i + t + 1)
                    if t % 2 == 0:
                        dve.wait_ge(s_u, 3 * pair + 2)
                        if not along_w:
                            dve.wait_ge(s_dcol, i + 1)
                            if t == 0 and not first:
                                dve.wait_ge(s_dz, 3 * i)
                        if not first:
                            dve.wait_ge(s_z, 3 * (pair - PAIRS) + 3)
                    nc.vector.tensor_tensor(hs[:, 0:2, t, :], wide_ps[:, :, 0:N], u[:, 0:2, t, :], ALU.add).then_inc(s_h_wide, 1)

                def shared_state(i, t):
                    dve.wait_ge(s_mm_shared, T * i + t + 1)
                    if t % 2 == 0:
                        dve.wait_ge(s_u, 3 * (PAIRS * i + t // 2) + 3)
                    nc.vector.tensor_tensor(hs[:, 2, t, :], shared_ps[:, 0:N], u[:, 2, t, :], ALU.add).then_inc(s_h_shared, 1)

                def make_z(i, P, j, early):
                    q = P % PAIRS
                    dve.wait_ge(s_h_wide if j < 2 else s_h_shared, 2 * (PAIRS * i + P) + 2)
                    cv = v_scan[:, j, V_CV:V_CV + 1]
                    src = hs[:, j, 2 * q:2 * q + 2, 0:W]
                    dst = z[:, j, 2 * q:2 * q + 2, :]
                    if along_w:
                        nc.vector.scalar_tensor_tensor(dst, src, cv, dst, ALU.mult, ALU.add).then_inc(s_z, 1)
                    else:
                        if not early and j == 0:
                            dve.wait_ge(s_zt, HT * (2 * (PAIRS * i + P - PAIRS) + 2))
                        nc.vector.tensor_scalar(dst, src, cv, None, ALU.mult).then_inc(s_z, 1)

                def add_part(i, t):
                    slot = (t // G) % 2
                    for h in range(HT):
                        dve.wait_ge(s_zt, HT * (T * i + t) + h + 1)
                        if h == 0 and t % G == 0:
                            dve.wait_ge(s_part[slot], 32 * (i + 1))
                        dst = step_tile(os[slot], t % G, h)
                        nc.vector.tensor_tensor(dst, pixels_first(h), dst, ALU.add).then_inc(s_out, 1)

                def diag_in(i):
                    nc.vector.tensor_scalar(u[:, :, :, W:W + 2], u_diag[:, :, bass.ds(T * i, T), :], 1.0, None, ALU.mult).then_inc(s_dcol, 1)

                def diag_out(i):
                    dve.wait_ge(s_h_wide, T * (i + 1))
                    dve.wait_ge(s_h_shared, T * (i + 1))
                    for j in range(3):
                        nc.vector.tensor_scalar(z_diag[:, j, bass.ds(T * i, T), :], hs[:, j, :, W:W + 2], v_scan[:, j, V_CV:V_CV + 1],
                                                None, ALU.mult).then_inc(s_dz, 1)

                if not along_w:
                    diag_in(0)

                def body(i, first, last):
                    for t in range(T):
                        wide_state(i, t, first)
                        shared_state(i, t)
                        if t % 2 == 1:
                            for j in range(2):
                                make_z(i, t // 2, j, first)
                        elif not (first and t == 0):
                            make_z(i, t // 2 - 1, 2, first)
                        if along_w and not (first and t < 3):
                            add_part(i, t - 3)
                    if not along_w:
                        diag_out(i)
                        if not last:
                            diag_in(i + 1)
                loop(dve, H // T, body)
                last = H // T - 1
                make_z(last, PAIRS - 1, 2, False)
                if along_w:
                    for t in range(T - 3, T):
                        add_part(last, t)

        if not along_w:
            s_fix = [sem("fix_" + n) for n in ("sum", "load", "zt", "add", "store")]
            s_sum, s_fload, s_fzt, s_add, s_fst = s_fix
            with nc.Block() as block:
                @block.sync
                def _(sp):
                    for b in range(B):
                        for d in range(2):
                            for h in range(HT):
                                sp.dma_start(px_diag[:, d, h, C * b:C * b + C], diagonal(part_d[b], d, h)).then_inc(s_fload, 16)
                    for d in range(2):
                        for h in range(HT):
                            sp.wait_ge(s_add, HT * d + h + 1)
                            for b in range(B):
                                sp.dma_start(diagonal(part_d[b], d, h), px_diag[:, d, h, C * b:C * b + C]).then_inc(s_fst, 16)
                    sp.wait_ge(s_fst, 16 * B * 2 * HT)

                @block.vector
                def _(dve):
                    nc.vector.tensor_tensor(z_diag[:, :, :, :], z_diag[:, :, :, :], e_diag[:, :, :, :], ALU.add).then_inc(s_sum, 1)
                    dve.wait_ge(s_fload, 16 * B * 2 * HT)
                    for d in range(2):
                        for h in range(HT):
                            dve.wait_ge(s_fzt, HT * d + h + 1)
                            dst = px_diag[:, d, h, :].rearrange("p (b c) -> p b c", b=B)
                            nc.vector.tensor_tensor(dst, pixels_first(h), dst, ALU.add).then_inc(s_add, 1)

                @block.tensor
                def _(pe):
                    pe.wait_ge(s_sum, 1)
                    for d in range(2):
                        for h in range(HT):
                            if d > 0:
                                pe.wait_ge(s_add, HT * (d - 1) + h + 1)
                            for j in range(3):
                                ins = nc.tensor.transpose(channels(pixels_first(h), j), z_diag[:, j, 128 * h:128 * h + 128, d], ident)
                            ins.then_inc(s_fzt, 1)


def kernel(x, L0_conv_w_qkv, L0_conv_b_qkv, L0_conv_w_dw, L0_conv_b_dw, L0_conv_temperature, L0_conv_w_out, L0_conv_b_out,
           L1_conv_A, L1_conv_Bv, L1_conv_Cv, L1_conv_Dv, L1_conv_res_scale):
    import concourse.bacc as bacc
    from concourse.bass_utils import run_bass_kernel_spmd

    x = np.asarray(x)
    nb, H, W, nch = x.shape
    x_cm = np.zeros((B, C, H + 1, W), np.float32)
    x_cm[:, :, :H] = x.transpose(0, 3, 1, 2)

    x_px = np.concatenate([x[0], x[1, :, :, 128:], x[1, :, :, :128]], axis=-1).reshape(H * W, B * C)

    w_dw, b_qkv, b_dw = (np.asarray(a) for a in (L0_conv_w_dw, L0_conv_b_qkv, L0_conv_b_dw))
    rows = np.concatenate([w_dw.reshape(9, 3 * C), b_qkv[None], b_dw[None]]).T
    last = rows[512:576]
    vec128 = np.stack([rows[0:128], rows[128:256], rows[256:384], rows[384:512], np.concatenate([last, last])], axis=1)

    temp = np.repeat(np.asarray(L0_conv_temperature).reshape(4), C // 4)
    res_scale = np.repeat(np.asarray(L1_conv_res_scale), C)
    cols = [L1_conv_Bv, L1_conv_Cv, L1_conv_Dv, L0_conv_b_out, res_scale, temp]
    vec96 = np.stack([np.asarray(c).reshape(2, KC) for c in cols], axis=-1).transpose(1, 0, 2)

    per_channel = np.stack([np.asarray(c).reshape(C) for c in (L1_conv_Bv, L1_conv_Cv, L1_conv_Dv, L0_conv_b_out, res_scale)], axis=-1)
    last = per_channel[128:]
    vec_scan = np.stack([per_channel[:128], per_channel[:128], np.concatenate([last, last])], axis=1)
    A = np.asarray(L1_conv_A)
    a_mat = np.zeros((128, 4, 128), np.float32)
    a_mat[:, 0] = A[:128, :128]
    for b in range(B):
        rows = slice((C - 128) * b, (C - 128) * (b + 1))
        a_mat[rows, 1] = A[128:, :128]
        a_mat[rows, 2, rows] = A[128:, 128:]
    a_mat[:, 3, :C - 128] = A[:128, 128:]

    ch = np.arange(KC)
    select = np.eye(384, dtype=np.float32).reshape(3, 128, 384).transpose(1, 0, 2)
    gavg = ((ch[:, None] // GROUP) == (ch[None] // GROUP)).astype(np.float32) / np.float32(GROUP)
    mask = np.where((ch[:, None] // 48) == (ch[None] // 48), 0.0, -1e30).astype(np.float32)

    def halves(w):
        return np.asarray(w).reshape(2, KC, -1).transpose(1, 0, 2)

    inputs = dict(x_cm=x_cm.reshape(B, C, (H + 1) * W), x_px=x_px, w_qkv=halves(L0_conv_w_qkv), w_out=halves(L0_conv_w_out),
                  a_mat=a_mat, vec128=vec128, vec96=vec96, vec_scan=vec_scan, select=select, gavg_d=gavg, mask_d=mask)
    inputs = {k: np.ascontiguousarray(v) for k, v in inputs.items()}
    nc = bacc.Bacc("TRN2", target_bir_lowering=False, num_devices=1)
    aps = {k: nc.dram_tensor(k, list(v.shape), F32, kind="ExternalInput").ap() for k, v in inputs.items()}
    x1_d = nc.dram_tensor("x1_d", [H * W, B * C], F32, kind="Internal").ap()
    part_d = nc.dram_tensor("part_d", [B, H * W, C], F32, kind="Internal").ap()
    out = nc.dram_tensor("out", [B, H * W, C], F32, kind="ExternalOutput").ap()
    build(nc, **aps, x1_d=x1_d, part_d=part_d, out=out, H=H, W=W)
    r = run_bass_kernel_spmd(nc, [inputs], core_ids=[0])
    return r.results[0]["out"].reshape(B, H, W, C)
```
